# Optimizing a Trainium2 kernel written in Bass

```python
import numpy as np
import jax
import jax.numpy as jnp

def _softmax(x, axis=-1):
    return jax.nn.softmax(x, axis=axis)

def _gelu(x):
    return jax.nn.gelu(x, approximate=True)

def _silu(x):
    return jax.nn.silu(x)

def _sigmoid(x):
    return jax.nn.sigmoid(x)

def _layernorm(x, axis=-1, eps=1e-05):
    m = jnp.mean(x, axis=axis, keepdims=True)
    v = jnp.var(x, axis=axis, keepdims=True)
    return (x - m) / jnp.sqrt(v + eps)

def _scatter_add(tgt, idx, src, axis=0):
    return tgt.at[idx].add(src)

def _segment_sum(src, seg, n):
    return jax.ops.segment_sum(src, seg, n)
kernel_name = 'mk_gnn_resnorm_d2_gnn_r8_18dec5'

def setup_inputs(seed: int=0):
    np.random.seed(seed)
    _w = jnp.asarray

    def _rec_inputs():
        import jax
        import jax.numpy as jnp
        _gk = jax.random.key(seed)
        x = 0.0001712 + 1 * jax.random.normal(jax.random.fold_in(_gk, 1), (12500, 16), jnp.float32)
        src = jax.random.randint(jax.random.fold_in(_gk, 2), (400000,), 0, 12500, jnp.int32)
        dst = jax.random.randint(jax.random.fold_in(_gk, 3), (400000,), 0, 12500, jnp.int32)
        _o = jnp.argsort(dst, stable=True)
        src = src[_o]
        dst = dst[_o]
        edge_attr_16 = 2.32446e-05 + 1 * jax.random.normal(jax.random.fold_in(_gk, 12), (400000, 16), jnp.float32)
        edge_type_8 = jax.random.randint(jax.random.fold_in(_gk, 13), (400000,), 0, 8, jnp.int32)
        return (x, src, dst, edge_attr_16, edge_type_8)
    x, src, dst, edge_attr_16, edge_type_8 = _rec_inputs()

    def _L0_gnn_setup():
        import jax, jax.numpy as jnp
        import numpy as np
        N_NODES = 6250
        N_EDGES = 62500
        IN_F = 16
        OUT_F = 16
        E_DIM = 16
        key = jax.random.key(seed)
        k1, k2, k3, k4, k5 = jax.random.split(key, 5)
        feat = jax.random.normal(k1, (N_NODES, IN_F), dtype=jnp.float32)
        efeat = jax.random.normal(k2, (N_EDGES, E_DIM), dtype=jnp.float32)
        W_e = jax.random.normal(k3, (E_DIM, IN_F * OUT_F), dtype=jnp.float32) * (1.0 / np.sqrt(E_DIM))
        b_e = jnp.zeros((IN_F * OUT_F,), dtype=jnp.float32)
        bias = jnp.zeros((OUT_F,), dtype=jnp.float32)
        src = jax.random.randint(k4, (N_EDGES,), 0, N_NODES, dtype=jnp.int32)
        dst = jax.random.randint(k5, (N_EDGES,), 0, N_NODES, dtype=jnp.int32)
        return {'feat': feat, 'efeat': efeat, 'W_e': W_e, 'b_e': b_e, 'bias': bias, 'src': src, 'dst': dst}
    _L0_gnn_all = _L0_gnn_setup()
    _L0_gnn_in = {k: v for k, v in _L0_gnn_all.items() if k in ('W_e', 'b_e', 'bias')}
    del _L0_gnn_all

    def _L1_gnn_setup():
        import jax, jax.numpy as jnp
        import numpy as np
        N_NODES = 12500
        N_EDGES = 125000
        MSG_DIM = 16
        HID_DIM = 16
        N_EDGE_TYPE = 8
        key = jax.random.key(seed)
        ks = jax.random.split(key, 9)
        features = jax.random.normal(ks[0], (N_NODES, HID_DIM), dtype=jnp.float32)
        edge_src = jax.random.randint(ks[1], (N_EDGES,), 0, N_NODES, dtype=jnp.int32)
        edge_dst = jax.random.randint(ks[2], (N_EDGES,), 0, N_NODES, dtype=jnp.int32)
        edge_type = jax.random.randint(ks[3], (N_EDGES,), 0, N_EDGE_TYPE, dtype=jnp.int32)
        edge_emb = jax.random.normal(ks[4], (N_EDGE_TYPE, MSG_DIM * HID_DIM), dtype=jnp.float32) * 0.1
        s = 1.0 / np.sqrt(HID_DIM)
        w_ih = jax.random.uniform(ks[5], (3 * HID_DIM, MSG_DIM), minval=-s, maxval=s, dtype=jnp.float32)
        w_hh = jax.random.uniform(ks[6], (3 * HID_DIM, HID_DIM), minval=-s, maxval=s, dtype=jnp.float32)
        b_ih = jax.random.uniform(ks[7], (3 * HID_DIM,), minval=-s, maxval=s, dtype=jnp.float32)
        b_hh = jax.random.uniform(ks[8], (3 * HID_DIM,), minval=-s, maxval=s, dtype=jnp.float32)
        return {'features': features, 'edge_src': edge_src, 'edge_dst': edge_dst, 'edge_type': edge_type, 'edge_emb': edge_emb, 'w_ih': w_ih, 'w_hh': w_hh, 'b_ih': b_ih, 'b_hh': b_hh}
    _L1_gnn_all = _L1_gnn_setup()
    _L1_gnn_in = {k: v for k, v in _L1_gnn_all.items() if k in ('edge_emb', 'w_ih', 'w_hh', 'b_ih', 'b_hh')}
    del _L1_gnn_all
    return {'x': x, 'src': src, 'dst': dst, 'edge_attr_16': edge_attr_16, 'edge_type_8': edge_type_8, 'L0_gnn_W_e': _L0_gnn_in['W_e'], 'L0_gnn_b_e': _L0_gnn_in['b_e'], 'L0_gnn_bias': _L0_gnn_in['bias'], 'L1_gnn_edge_emb': _L1_gnn_in['edge_emb'], 'L1_gnn_w_ih': _L1_gnn_in['w_ih'], 'L1_gnn_w_hh': _L1_gnn_in['w_hh'], 'L1_gnn_b_ih': _L1_gnn_in['b_ih'], 'L1_gnn_b_hh': _L1_gnn_in['b_hh']}

def reference(x, src, dst, edge_attr_16, edge_type_8, L0_gnn_W_e, L0_gnn_b_e, L0_gnn_bias, L1_gnn_edge_emb, L1_gnn_w_ih, L1_gnn_w_hh, L1_gnn_b_ih, L1_gnn_b_hh):
    import jax
    import jax.numpy as jnp

    def _L0_gnn_ref(feat, efeat, W_e, b_e, bias, src, dst):
        import jax, jax.numpy as jnp
        import numpy as np
        N_NODES = 6250
        N_EDGES = 62500
        IN_F = 16
        OUT_F = 16
        E_DIM = 16
        E = efeat.shape[0]
        N, in_f = feat.shape
        out_f = bias.shape[0]
        ew = (efeat @ W_e + b_e).reshape(E, in_f, out_f)
        msg = jnp.einsum('ei,eio->eo', feat[src], ew)
        summed = jax.ops.segment_sum(msg, dst, num_segments=N)
        cnt = jax.ops.segment_sum(jnp.ones((E,), feat.dtype), dst, num_segments=N)
        neigh = summed / jnp.maximum(cnt, 1.0)[:, None]
        return neigh + bias

    def _L1_gnn_ref(features, edge_src, edge_dst, edge_type, edge_emb, w_ih, w_hh, b_ih, b_hh):
        import jax, jax.numpy as jnp
        import numpy as np
        N_NODES = 12500
        N_EDGES = 125000
        MSG_DIM = 16
        HID_DIM = 16
        N_EDGE_TYPE = 8
        n_nodes = features.shape[0]
        A = edge_emb[edge_type].reshape(-1, MSG_DIM, HID_DIM)
        h_src = features[edge_src]
        msg = jnp.einsum('emh,eh->em', A, h_src)
        m = jax.ops.segment_sum(msg, edge_dst, num_segments=n_nodes)
        gi = m @ w_ih.T + b_ih
        gh = features @ w_hh.T + b_hh
        i_r, i_z, i_n = jnp.split(gi, 3, axis=-1)
        h_r, h_z, h_n = jnp.split(gh, 3, axis=-1)
        r = jax.nn.sigmoid(i_r + h_r)
        z = jax.nn.sigmoid(i_z + h_z)
        n = jnp.tanh(i_n + r * h_n)
        h_new = (1.0 - z) * n + z * features
        return h_new
    x = _layernorm(x + _L0_gnn_ref(x, edge_attr_16, L0_gnn_W_e, L0_gnn_b_e, L0_gnn_bias, src, dst), axis=-1)
    x = _layernorm(x + _L1_gnn_ref(x, src, dst, edge_type_8, L1_gnn_edge_emb, L1_gnn_w_ih, L1_gnn_w_hh, L1_gnn_b_ih, L1_gnn_b_hh), axis=-1)
    return x

_drawn_inputs = setup_inputs


def setup_inputs(seed=0):
    import zlib

    import numpy as np

    out = dict(_drawn_inputs(seed))
    spreads = {'L0_gnn_b_e': (0.0, 0.1), 'L0_gnn_bias': (0.0, 0.1)}
    factors = {}
    for name, (base, spread) in spreads.items():
        noise = np.random.default_rng([zlib.crc32(name.encode()), seed]).standard_normal(out[name].shape)
        drawn = base * np.exp(spread * noise) if base else spread * noise
        out[name] = jnp.asarray(drawn.astype(out[name].dtype))
    for name, factor in factors.items():
        out[name] = (out[name] * factor).astype(out[name].dtype)
    return out
```

```python
import concourse.bass as bass
from concourse import mybir

P = 128
F = 16
K2 = F * F
ALU = mybir.AluOpType
ACT = mybir.ActivationFunctionType
AX = mybir.AxisListType
F32 = mybir.dt.float32
I32 = mybir.dt.int32

G = 25
CH = 5
NCH = G // CH
BLK = P * G
LOG_P = 7


def build(nc, x, src, dst, ea, etype, W_e, b_e, bias, A_t, w_ihT, w_hhT, b_ih, b_hh, out):
    N, E = x.shape[0], src.shape[0]
    T = A_t.shape[0] // F
    NB = E // BLK
    assert NB * BLK == E and NB % 2 == 1 and NB <= P and T * F == P
    R = 125
    C = N // R
    assert R * C == N
    ZW = K2 + 1 + F
    NPAD = N + P
    AGG1 = 32
    ROWS1 = AGG1 + F
    n_gate = -(-C // 8)
    GC = 4 * F
    PB = 512

    h_dram = nc.dram_tensor("h_rows", [N, F], F32, kind="Internal").ap()
    span_dram = nc.dram_tensor("block_span", [NB, 2], I32, kind="Internal").ap()

    from contextlib import ExitStack
    with ExitStack() as ctx:
        def sb(name, shape, dt=F32):
            return ctx.enter_context(nc.sbuf_tensor(name, shape, dt))[tuple(slice(None) for _ in shape)]

        def ps(name, shape):
            return ctx.enter_context(nc.psum_tensor(name, shape, F32))[tuple(slice(None) for _ in shape)]

        def sem(name):
            return ctx.enter_context(nc.semaphore(name))

        nodeT = sb("nodeT", [ROWS1, NPAD])
        z = [sb(f"z{b}", [P, G, ZW]) for b in range(2)]
        onehot = sb("onehot", [P, G, P])
        xs = [sb(f"xs{b}", [P, G, F]) for b in range(2)]
        idx = [sb(f"idx{b}", [P, G], I32) for b in range(2)]
        dstb = [sb(f"dstb{b}", [P, G], I32) for b in range(2)]
        eab = [sb(f"eab{b}", [P, G, F]) for b in range(2)]
        typ = [sb(f"typ{b}", [P, G], I32) for b in range(2)]
        typ_hot = sb("typ_hot", [P, G, T])
        rel = sb("rel", [P, G])
        dst_rows = sb("dst_rows", [NB, BLK], I32)
        span = sb("span", [NB, 2], I32)
        span_hi = sb("span_hi", [NB, 1], I32)
        span_row = sb("span_row", [1, NB, 2], I32)
        ones_row = sb("ones_row", [1, NB])
        win_f = sb("win_f", [1, NB])
        win_sum = sb("win_sum", [1, NB + 1])
        win_first = sb("win_first", [1, NB + 1], I32)
        lo_i = sb("lo_i", [P, NB, 2], I32)
        lo_f = sb("lo_f", [P, NB])
        col_i = sb("col_i", [P, P], I32)
        col_f = sb("col_f", [P, P])
        ident = sb("ident", [P, P])
        sumS = sb("sumS", [P, ZW])
        sumT = sb("sumT", [P, 3, P])
        W0 = sb("W0", [P, 3, F + 1])
        A1 = sb("A1", [P, ROWS1])
        gate_w = sb("gate_w", [ROWS1, GC])
        bias_b = sb("bias_b", [R, F])
        xn = sb("xn", [R, C, F])
        h = sb("h", [R, C, 2 * F])
        ya = sb("ya", [R, C, F])
        yb = sb("yb", [R, C, F])
        rz = sb("rz", [R, C, 2 * F])
        st = [sb(f"st{k}", [R, C]) for k in range(4)]
        eps = sb("eps", [R, 1])

        psM = ps("psM", [P, PB])
        psT = ps("psT", [P, PB])
        psR = ps("psR", [P, PB])
        psN = ps("psN", [P, 5, PB])

        s_w = sem("s_w")
        s_w0z = sem("s_w0z")
        s_const = sem("s_const")
        s_colf = sem("s_colf")
        s_dr = sem("s_dr")
        s_v = sem("s_v")
        s_span = sem("s_span")
        s_var = sem("s_var")
        s_spd = sem("s_spd")
        s_spr = sem("s_spr")
        s_meta = sem("s_meta")
        s_init = sem("s_init")
        s_agg = [sem(f"s_agg{k}") for k in range(2)]
        s_nt = sem("s_nt")
        s_nv = sem("s_nv")
        s_a = sem("s_a")
        s_h = sem("s_h")
        s_hd = sem("s_hd")
        s_ht = sem("s_ht")
        s_hc = sem("s_hc")
        s_g = sem("s_g")
        s_sig = sem("s_sig")
        s_gn = sem("s_gn")
        s_out = sem("s_out")
        s_turn = sem("s_turn")
        s_done = sem("s_done")
        L = []
        for k in range(2):
            L.append(dict(
                inp=[sem(f"l{k}_in{b}") for b in range(2)],
                got=[[sem(f"l{k}_got{b}_{j}") for j in range(NCH)] for b in range(2)],
                z=sem(f"l{k}_z"), x=sem(f"l{k}_x"), hot=sem(f"l{k}_hot"), rel=sem(f"l{k}_rel"),
                match=sem(f"l{k}_match"), mm=sem(f"l{k}_mm"), mS=sem(f"l{k}_mS"),
                tp=sem(f"l{k}_tp"), tS=sem(f"l{k}_tS"), res=sem(f"l{k}_res"), acc=sem(f"l{k}_acc")))
        CREDIT = 2 * NCH

        def cols(t, c):
            return t[:, c:N:C]

        def for_each_block(eng, body):
            with eng.Fori(0, NB // 2) as i:
                for b in range(2):
                    body(2 * i + b, b, i)
            body(NB - 1, 0, NB // 2)

        def windows_of(eng, b):
            n_win = eng.value_load(span_row[0:1, bass.ds(b, 1), 1:2].rearrange("p a b -> p (a b)"),
                                   min_val=1, max_val=(N - 1) // P + 1)
            first = eng.value_load(win_first[0:1, bass.ds(b, 1)], min_val=0, max_val=NB * P)
            return first, n_win

        def for_each_window(eng, first, n_win, body):
            with eng.Fori(0, n_win) as q:
                body(first + q, q)

        block = ctx.enter_context(nc.Block())

        @block.sync
        def _(sp):
            blk = lambda a, b: a[bass.ds(b * BLK, BLK)].rearrange("(p g) -> p g", g=G)

            def load(k, b, buf):
                s = L[k]["inp"][buf]
                sp.dma_start(idx[buf][:], blk(src, b)).then_inc(s, 16)
                sp.dma_start(dstb[buf][:], blk(dst, b)).then_inc(s, 16)
                if k == 0:
                    sp.dma_start(eab[buf][:], ea[bass.ds(b * BLK, BLK), :].rearrange("(p g) f -> p g f", g=G)).then_inc(s, 16)
                else:
                    sp.dma_start(typ[buf][:], blk(etype, b)).then_inc(s, 16)

            def edge_loads(k):
                used = L[k]["z"]
                with sp.Fori(0, NB // 2 - 1) as i:
                    for buf in range(2):
                        sp.wait_ge(used, CREDIT + NCH * (2 * i + buf + 1))
                        load(k, 2 * i + buf + 2, buf)
                sp.wait_ge(used, CREDIT + NCH * (NB - 2))
                load(k, NB - 1, 0)

            load(0, 0, 0)
            load(0, 1, 1)
            sp.dma_start(dst_rows[:], dst.rearrange("(b e) -> b e", e=BLK)).then_inc(s_dr, 16)
            sp.wait_ge(s_span, 1)
            sp.dma_start(span_dram, span[:]).then_inc(s_spd, 16)
            sp.wait_ge(s_spd, 16)
            sp.dma_start(span_row[:], span_dram.rearrange("(a b) c -> a b c", a=1)).then_inc(s_spr, 16)
            sp.dma_start(lo_i[:], span_dram.partition_broadcast(P)).then_inc(s_spr, 16)
            sp.wait_ge(s_w0z, 3)
            sp.dma_start(W0[:, 0, 0:F], W_e[0:P, :]).then_inc(s_w, 16)
            sp.dma_start(W0[:, 1, 0:F], W_e[P:2 * P, :]).then_inc(s_w, 16)
            sp.dma_start(W0[1:1 + F, 2, 0:F], b_e).then_inc(s_w, 16)
            sp.dma_start(A1[:, AGG1:ROWS1], A_t).then_inc(s_w, 16)
            sp.dma_start(gate_w[0:F, 0:2 * F], w_hhT[:, 0:2 * F]).then_inc(s_w, 16)
            sp.dma_start(gate_w[0:F, 3 * F:GC], w_hhT[:, 2 * F:3 * F]).then_inc(s_w, 16)
            sp.dma_start(gate_w[F:F + 1, 0:3 * F], b_ih).then_inc(s_w, 16)
            sp.dma_start(gate_w[F + 1:F + 2, 0:2 * F], b_hh[:, 0:2 * F]).then_inc(s_w, 16)
            sp.dma_start(gate_w[F + 1:F + 2, 3 * F:GC], b_hh[:, 2 * F:3 * F]).then_inc(s_w, 16)
            sp.dma_start(gate_w[AGG1:ROWS1, 0:3 * F], w_ihT).then_inc(s_w, 16)
            sp.dma_start(bias_b[:], bias[0, :].partition_broadcast(R)).then_inc(s_w, 16)
            sp.dma_start(xn[:], x.rearrange("(r c) f -> r c f", c=C)).then_inc(s_w, 16)
            edge_loads(0)
            sp.wait_ge(s_h, 1)
            sp.dma_start(h_dram.rearrange("(r c) f -> r c f", c=C), h[:, :, 0:F]).then_inc(s_hd, 16)
            load(1, 0, 0)
            load(1, 1, 1)
            edge_loads(1)
            sp.wait_ge(s_out, 1)
            sp.dma_start(out.rearrange("(r c) f -> r c f", c=C), yb[:]).then_inc(s_done, 16)
            sp.wait_ge(s_done, 16)
        N_W = 12 * 16

        @block.gpsimd
        def _(pool):
            def gathers(k, table):
                l = L[k]

                def body(b, buf, r):
                    pool.wait_ge(l["inp"][buf], 48 * (r + 1))
                    if k == 0:
                        pool.wait_ge(l["x"], b + 1)
                    for j in range(NCH):
                        pool.wait_ge(l["z"], NCH * b + j + 1)
                        pool.sem_inc(s_turn)
                        for g in range(j * CH, j * CH + CH):
                            pool.indirect_dma_start(
                                xs[buf][:, g, :], None, table,
                                bass.IndirectOffsetOnAxis(ap=idx[buf][:, g:g + 1], axis=0),
                            ).then_inc(l["got"][buf][j], 16)
                for_each_block(pool, body)

            pool.iota(col_i[:], [[1, P]], base=0, channel_multiplier=0).then_inc(s_const, 1)
            pool.memset(ident[:], 0.0).then_inc(s_const, 1)
            pool.wait_ge(s_const, 2)
            pool.affine_select(out=ident[:], in_=ident[:], compare_op=ALU.not_equal, fill=1.0, base=0,
                               pattern=[[-1, P]], channel_multiplier=1).then_inc(s_const, 1)
            gathers(0, x)
            pool.wait_ge(s_hd, 16)
            gathers(1, h_dram)

        @block.scalar
        def _(act):
            def evacuate(k):
                l = L[k]

                def body(b, buf, r):
                    if k == 0:
                        for j in range(NCH):
                            act.wait_ge(l["got"][buf][j], 16 * CH * (r + 1))
                        act.copy(z[buf][:, :, K2 + 1:ZW], xs[buf][:]).then_inc(l["x"], 1)

                    def window(w, q):
                        act.wait_ge(l["mm"], w + 1)
                        W = ZW if k == 0 else P
                        act.copy(sumS[:, 0:W], psM[:, 0:W]).then_inc(l["mS"], 1)
                        act.wait_ge(l["tp"], w + 1)
                        if k == 0:
                            act.copy(sumT[0:F + 1, 2, :], psT[0:F + 1, 2 * P:3 * P]).then_inc(l["tS"], 1)
                            act.copy(sumT[:, 0:2, :].rearrange("p a b -> p (a b)"), psT[:, 0:2 * P]).then_inc(l["tS"], 1)
                        else:
                            act.copy(sumT[:, 0, :], psT[:, 0:P]).then_inc(l["tS"], 2)
                    for_each_window(act, *windows_of(act, b), window)
                for_each_block(act, body)

            act.sem_inc(L[0]["x"], 2)
            act.wait_ge(s_init, 2)
            act.wait_ge(s_meta, 1)
            evacuate(0)
            act.wait_ge(s_var, 1)
            act.activation(st[2][:], st[1][:], ACT.Sqrt, bias=eps[:, 0:1], scale=1.0 / F).then_inc(s_a, 1)
            for g in range(C // 4):
                act.wait_ge(s_ht, g + 1)
                v = nodeT[0:2 * F, 0:N].rearrange("f (r c) -> f c r", c=C)[:, 4 * g:4 * g + 4, :]
                act.copy(v, psN[0:2 * F, g % 5, 0:4 * R].rearrange("f (c r) -> f c r", r=R)).then_inc(s_hc, 1)
            evacuate(1)
            for g in range(n_gate):
                c0, c1 = 8 * g, min(8 * g + 8, C)
                act.wait_ge(s_g, g + 1)
                act.activation(rz[:, c0:c1, :],
                               psN[0:R, g % 5, 0:GC * (c1 - c0)].rearrange("r (c k) -> r c k", k=GC)[:, :, 0:2 * F],
                               ACT.Sigmoid).then_inc(s_sig, 1)
                act.wait_ge(s_gn, 2 * g + 2)
                act.activation(ya[:, c0:c1, :], ya[:, c0:c1, :], ACT.Tanh).then_inc(s_a, 1)
            act.wait_ge(s_var, 2)
            act.activation(st[2][:], st[1][:], ACT.Sqrt, bias=eps[:, 0:1], scale=1.0 / F).then_inc(s_a, 1)

        @block.tensor
        def _(pe):
            def sums(k):
                l = L[k]
                W = ZW if k == 0 else P

                def body(b, buf, r):
                    if k == 0:
                        pe.wait_ge(l["x"], b + 3)

                    def window(w, q):
                        pe.wait_ge(l["match"], w + 1)
                        for g in range(G):
                            mm = pe.matmul(psM[:, 0:W], onehot[:, g, :], z[buf][:, g, 0:W],
                                           start=(g == 0), stop=(g == G - 1))
                        mm.then_inc(l["mm"], 1)
                        pe.wait_ge(l["mS"], w + 1)
                        if k == 0:
                            for c in range(2):
                                pe.transpose(psT[:, c * P:c * P + P], sumS[:, c * P:c * P + P], ident[:])
                            pe.transpose(psT[0:F + 1, 2 * P:3 * P], sumS[:, K2:ZW], ident[:]).then_inc(l["tp"], 1)
                            pe.wait_ge(l["tS"], 2 * w + 2)
                            for c in range(2):
                                pe.matmul(psR[0:F + 1, 0:P], W0[:, c, :], sumT[:, c, :], start=(c == 0), stop=False)
                            pe.matmul(psR[0:F + 1, 0:P], W0[0:F + 1, 2, :], sumT[0:F + 1, 2, :],
                                      start=False, stop=True).then_inc(l["res"], 1)
                        else:
                            pe.transpose(psT[:, 0:P], sumS[:, 0:P], ident[:]).then_inc(l["tp"], 1)
                            pe.wait_ge(l["tS"], 2 * w + 2)
                            pe.matmul(psR[0:ROWS1, 0:P], A1[:], sumT[:, 0, :], start=True, stop=True).then_inc(l["res"], 1)
                    for_each_window(pe, *windows_of(pe, b), window)
                for_each_block(pe, body)

            pe.wait_ge(s_const, 3)
            pe.wait_ge(s_w, N_W)
            pe.wait_ge(s_meta, 1)
            sums(0)
            pe.wait_ge(s_agg[0], 1)
            for g in range(5):
                for c in range(20 * g, 20 * g + 20):
                    t = pe.transpose(psN[0:R, g, (c - 20 * g) * (F + 1):(c - 20 * g + 1) * (F + 1)],
                                     cols(nodeT[0:F + 1, :], c), ident[0:F + 1, 0:F + 1])
                t.then_inc(s_nt, 1)
            pe.wait_ge(s_h, 1)
            for g in range(C // 4):
                if g >= 5:
                    pe.wait_ge(s_hc, g - 4)
                for c in range(4 * g, 4 * g + 4):
                    t = pe.transpose(psN[0:2 * F, g % 5, (c - 4 * g) * R:(c - 4 * g + 1) * R],
                                     h[:, c, :], ident[0:R, 0:R])
                t.then_inc(s_ht, 1)
            sums(1)
            pe.wait_ge(s_agg[1], 1)
            pe.wait_ge(s_hc, C // 4)
            for g in range(n_gate):
                if g >= 5:
                    pe.wait_ge(s_sig, g - 4)
                    pe.wait_ge(s_gn, 2 * (g - 4))
                for c in range(8 * g, min(8 * g + 8, C)):
                    t = pe.matmul(psN[0:R, g % 5, (c - 8 * g) * GC:(c - 8 * g + 1) * GC],
                                  cols(nodeT, c), gate_w[:], start=True, stop=True)
                t.then_inc(s_g, 1)

        @block.vector
        def _(dve):
            steps = [0]

            def step(ins):
                steps[0] += 1
                ins.then_inc(s_v, 1)
                dve.wait_ge(s_v, steps[0])

            def bc(t, n):
                return t.unsqueeze(2).to_broadcast([t.shape[0], t.shape[1], n])

            def aggregate(k):
                l = L[k]
                p0, p1 = (0, F + 1) if k == 0 else (AGG1, ROWS1)
                at = dve.alloc_register(f"window_at{k}")
                dve.reg_mov(at, 0)

                def add_window(w):
                    dve.wait_ge(l["res"], w + 1)
                    dve.wait_ge(l["acc"], w + 1)
                    v = nodeT[p0:p1, bass.ds(dve.snap(at, min_val=0, max_val=N - 1), P)]
                    dve.tensor_tensor(v, v, psR[p0:p1, 0:P], ALU.add).then_inc(l["acc"], 1)

                def body(b, buf, r):
                    first, n_win = windows_of(dve, b)
                    dve.wait_ge(l["inp"][buf], 48 * (r + 1))
                    dve.wait_ge(l["rel"], b + first + 1)
                    dve.tensor_scalar(rel[:], dstb[buf][:], lo_f[:, bass.ds(b, 1)], None, ALU.subtract).then_inc(l["rel"], 1)
                    if k == 1:
                        dve.tensor_tensor(typ_hot[:], col_f[:, 0:T].unsqueeze(1).to_broadcast([P, G, T]),
                                          bc(typ[buf], T), ALU.is_equal).then_inc(l["hot"], 1)
                        dve.wait_ge(l["hot"], b + 1)
                    coef, n = (eab[buf], F) if k == 0 else (typ_hot, T)
                    for j in range(NCH):
                        g = slice(j * CH, j * CH + CH)
                        dve.wait_ge(l["got"][buf][j], 16 * CH * (r + 1))
                        dve.tensor_tensor(
                            z[buf][:, g, 0:n * F].rearrange("p g (k i) -> p g k i", i=F),
                            coef[:, g, :].unsqueeze(3).to_broadcast([P, CH, n, F]),
                            xs[buf][:, g, :].unsqueeze(2).to_broadcast([P, CH, n, F]), ALU.mult).then_inc(l["z"], 1)
                    lo = dve.value_load(span_row[0:1, bass.ds(b, 1), 0:1].rearrange("p a b -> p (a b)"),
                                        min_val=0, max_val=N - 1)

                    def window(w, q):
                        add_window(w)
                        dve.reg_mov(at, lo + q * P)
                        dve.wait_ge(l["rel"], b + w + 2)
                        dve.tensor_tensor(onehot[:], col_f[:].unsqueeze(1).to_broadcast([P, G, P]),
                                          bc(rel, P), ALU.is_equal).then_inc(l["match"], 1)
                        dve.wait_ge(l["match"], w + 1)
                        dve.tensor_scalar(rel[:], rel[:], float(P), None, ALU.subtract).then_inc(l["rel"], 1)
                    for_each_window(dve, first, n_win, window)
                for_each_block(dve, body)
                last = dve.value_load(win_first[0:1, NB:NB + 1], min_val=1, max_val=NB * P)
                dve.wait_ge(l["res"], last + 1)
                dve.wait_ge(l["acc"], last + 1)
                v = nodeT[p0:p1, bass.ds(dve.snap(at, min_val=0, max_val=N - 1), P)]
                dve.tensor_tensor(v, v, psR[p0:p1, 0:P], ALU.add).then_inc(s_agg[k], 1)

            def centre_and_square():
                step(dve.tensor_reduce(st[0][:], ya[:], AX.X, ALU.add))
                step(dve.tensor_scalar(st[0][:], st[0][:], 1.0 / F, None, ALU.mult))
                step(dve.tensor_tensor(yb[:], ya[:], bc(st[0], F), ALU.subtract))
                step(dve.tensor_tensor(ya[:], yb[:], yb[:], ALU.mult))
                step(dve.tensor_reduce(st[1][:], ya[:], AX.X, ALU.add))
                dve.sem_inc(s_var, 1)

            dve.wait_ge(s_dr, 16)
            step(dve.tensor_reduce(span[:, 0:1], dst_rows[:], AX.X, ALU.min))
            step(dve.tensor_reduce(span_hi[:], dst_rows[:], AX.X, ALU.max))
            dve.tensor_tensor(span_hi[:], span_hi[:], span[:, 0:1], ALU.subtract).then_inc(s_init, 1)
            dve.wait_ge(s_init, 1)
            dve.tensor_scalar(span_hi[:], span_hi[:], LOG_P, None, ALU.arith_shift_right).then_inc(s_init, 1)
            dve.wait_ge(s_init, 2)
            step(dve.tensor_scalar(span[:, 1:2], span_hi[:], 1.0, None, ALU.add))
            dve.sem_inc(s_span, 1)

            dve.memset(W0[:], 0.0).then_inc(s_w0z, 1)
            dve.wait_ge(s_w0z, 1)
            dve.memset(W0[0:1, 2, F:F + 1], 1.0).then_inc(s_w0z, 1)
            dve.memset(A1[:], 0.0)
            dve.memset(gate_w[:], 0.0).then_inc(s_w0z, 1)
            dve.memset(ones_row[:], 1.0)
            dve.memset(win_sum[:], 0.0)
            dve.memset(eps[:], 1e-5)
            dve.memset(h[:], 0.0)
            dve.memset(nodeT[:], 0.0)
            step(dve.memset(psR[:], 0.0))
            for b in range(2):
                dve.memset(z[b][:, :, K2:K2 + 1], 1.0)
            step(dve.memset(h[:, :, F:F + 2], 1.0))
            dve.wait_ge(s_spr, 32)
            dve.tensor_copy(win_f[:], span_row[0:1, :, 1])
            dve.tensor_copy(lo_f[:], lo_i[:, :, 0])
            dve.wait_ge(s_const, 1)
            step(dve.tensor_copy(col_f[:], col_i[:]))
            step(dve.tensor_tensor_scan(win_sum[:, 1:NB + 1], ones_row[:], win_f[:], 0.0, ALU.mult, ALU.add))
            step(dve.tensor_copy(win_first[:], win_sum[:]))
            dve.sem_inc(s_meta, 1)
            for l in L:
                dve.sem_inc(l["z"], CREDIT)
                dve.sem_inc(l["res"], 1)
                dve.sem_inc(l["acc"], 1)
                dve.sem_inc(l["rel"], 1)

            aggregate(0)

            dve.wait_ge(s_w, N_W)
            step(dve.tensor_tensor(xn[:], xn[:], bias_b[:].unsqueeze(1).to_broadcast([R, C, F]), ALU.add))
            for g in range(5):
                dve.wait_ge(s_nt, g + 1)
                v = psN[0:R, g, 0:20 * (F + 1)].rearrange("r (c f) -> r c f", f=F + 1)
                cs = slice(20 * g, 20 * g + 20)
                step(dve.tensor_scalar(st[0][:, cs], v[:, :, F], 1.0, None, ALU.max))
                step(dve.reciprocal(st[0][:, cs], st[0][:, cs]))
                step(dve.tensor_tensor(ya[:, cs, :], v[:, :, 0:F], bc(st[0][:, cs], F), ALU.mult))
            step(dve.tensor_tensor(ya[:], ya[:], xn[:], ALU.add))
            centre_and_square()
            dve.wait_ge(s_a, 1)
            step(dve.reciprocal(st[3][:], st[2][:]))
            dve.tensor_tensor(h[:, :, 0:F], yb[:], bc(st[3], F), ALU.mult).then_inc(s_h, 1)
            step(dve.memset(psR[:], 0.0))

            aggregate(1)

            for g in range(n_gate):
                c0, c1 = 8 * g, min(8 * g + 8, C)
                v = psN[0:R, g % 5, 0:GC * (c1 - c0)].rearrange("r (c k) -> r c k", k=GC)
                dve.wait_ge(s_sig, g + 1)
                dve.tensor_tensor(ya[:, c0:c1, :], rz[:, c0:c1, 0:F], v[:, :, 3 * F:GC], ALU.mult).then_inc(s_gn, 1)
                dve.wait_ge(s_gn, 2 * g + 1)
                dve.tensor_tensor(ya[:, c0:c1, :], ya[:, c0:c1, :], v[:, :, 2 * F:3 * F], ALU.add).then_inc(s_gn, 1)
            dve.wait_ge(s_a, 1 + n_gate)
            hv = h[:, :, 0:F]
            step(dve.tensor_tensor(yb[:], hv, ya[:], ALU.subtract))
            step(dve.tensor_tensor(yb[:], yb[:], rz[:, :, F:2 * F], ALU.mult))
            step(dve.tensor_tensor(ya[:], ya[:], hv, ALU.add))
            step(dve.tensor_tensor(ya[:], ya[:], yb[:], ALU.add))
            centre_and_square()
            dve.wait_ge(s_a, 2 + n_gate)
            step(dve.reciprocal(st[3][:], st[2][:]))
            dve.tensor_tensor(yb[:], yb[:], bc(st[3], F), ALU.mult).then_inc(s_out, 1)


_INS = ["x", "src", "dst", "edge_attr_16", "edge_type_8", "W_e", "b_e", "bias", "A_t", "w_ihT", "w_hhT", "b_ih", "b_hh"]


def kernel(x, src, dst, edge_attr_16, edge_type_8, L0_gnn_W_e, L0_gnn_b_e, L0_gnn_bias, L1_gnn_edge_emb,
           L1_gnn_w_ih, L1_gnn_w_hh, L1_gnn_b_ih, L1_gnn_b_hh):
    import numpy as np
    import concourse.bacc as bacc
    from concourse.bass_utils import run_bass_kernel_spmd

    n_types = L1_gnn_edge_emb.shape[0]
    given = dict(
        x=x, src=src, dst=dst, edge_attr_16=edge_attr_16, edge_type_8=edge_type_8,
        W_e=np.asarray(L0_gnn_W_e).reshape(K2, F), b_e=np.asarray(L0_gnn_b_e).reshape(F, F),
        bias=np.asarray(L0_gnn_bias).reshape(1, F),
        A_t=np.asarray(L1_gnn_edge_emb).reshape(n_types, F, F).transpose(0, 2, 1).reshape(n_types * F, F),
        w_ihT=np.asarray(L1_gnn_w_ih).T, w_hhT=np.asarray(L1_gnn_w_hh).T,
        b_ih=np.asarray(L1_gnn_b_ih).reshape(1, 3 * F), b_hh=np.asarray(L1_gnn_b_hh).reshape(1, 3 * F))
    nc = bacc.Bacc("TRN2", target_bir_lowering=False, num_devices=1)
    arrays, args = {}, []
    for name in _INS:
        a = np.ascontiguousarray(given[name])
        arrays[f"in_{name}"] = a
        args.append(nc.dram_tensor(f"in_{name}", a.shape, mybir.dt.from_np(a.dtype), kind="ExternalInput").ap())
    args.append(nc.dram_tensor("out_0", x.shape, F32, kind="ExternalOutput").ap())
    build(nc, *args)
    r = run_bass_kernel_spmd(nc, [arrays], core_ids=[0])
    return r.results[0]["out_0"]
```

```python
import concourse.bass as bass
from concourse import mybir

P = 128
F = 16
K2 = F * F
ALU = mybir.AluOpType
ACT = mybir.ActivationFunctionType
AX = mybir.AxisListType
F32 = mybir.dt.float32
F32R = mybir.dt.float32r
I32 = mybir.dt.int32

G = 25
H_PE = (5, 7)
NCH = 5
TC = 8
BLK = P * G
LOG_P = 7


def chunk_cols(k):
    gp = G - H_PE[k]
    return [gp * j // (NCH - 1) for j in range(NCH)] + [G]


def build(nc, x, src, dst, ea, etype, W_e, b_e, bias, A_t, w_ihT, w_hhT, b_ih, b_hh, out):
    N, E = x.shape[0], src.shape[0]
    T = A_t.shape[0] // F
    NB = E // BLK
    assert NB * BLK == E and NB % 2 == 1 and NB <= P and T * F == P
    R = 125
    C = N // R
    assert R * C == N
    ZW = K2 + 1 + F
    NPAD = N + P
    AGG1 = 32
    ROWS1 = AGG1 + F
    NG = -(-N // (TC * P))
    HM = max(H_PE)
    n_gate = -(-C // 8)
    GC = 4 * F
    PB = 512

    h_dram = nc.dram_tensor("h_rows", [N, F], F32, kind="Internal").ap()
    span_dram = nc.dram_tensor("block_span", [NB, 2], I32, kind="Internal").ap()

    from contextlib import ExitStack
    with ExitStack() as ctx:
        def sb(name, shape, dt=F32):
            return ctx.enter_context(nc.sbuf_tensor(name, shape, dt))[tuple(slice(None) for _ in shape)]

        def ps(name, shape):
            return ctx.enter_context(nc.psum_tensor(name, shape, F32))[tuple(slice(None) for _ in shape)]

        def sem(name):
            return ctx.enter_context(nc.semaphore(name))

        nodeT = sb("nodeT", [ROWS1, NPAD])
        z_mem = [sb(f"z{b}", [P, G * ZW]) for b in range(2)]
        z = [m.rearrange("p (g c) -> p g c", c=ZW) for m in z_mem]
        onehot = sb("onehot", [P, G, P])
        srcb = [sb(f"srcb{b}", [P, HM * P], I32) for b in range(2)]
        src_mod = sb("src_mod", [P, HM * P], I32)
        pick = sb("pick", [P, TC, HM * P], F32R)
        chunk_node_i = sb("chunk_node_i", [P, TC], I32)
        chunk_node = sb("chunk_node", [P, TC])
        table_p = [sb(f"table_{n}", [P, TC * NG * F], F32R) for n in ("hi", "lo")]
        grp = sb("grp", [P, HM], I32)
        grp_hot = sb("grp_hot", [P, HM, NG])
        cand = sb("cand", [P, HM, NG, F])
        xs = [sb(f"xs{b}", [P, G, F]) for b in range(2)]
        idx = [sb(f"idx{b}", [P, G], I32) for b in range(2)]
        dstb = [sb(f"dstb{b}", [P, G], I32) for b in range(2)]
        eab = [sb(f"eab{b}", [P, G, F]) for b in range(2)]
        typ = [sb(f"typ{b}", [P, G], I32) for b in range(2)]
        typ_hot = sb("typ_hot", [P, G, T])
        rel = sb("rel", [P, G])
        t0, t1 = BLK, BLK + TC * NG * F
        table = z_mem[0][:, t0:t1].rearrange("p (c g f) -> p c g f", c=TC, f=F)
        dst_rows = z_mem[0][0:NB, 0:BLK].bitcast(I32)
        span = sb("span", [NB, 2], I32)
        span_hi = sb("span_hi", [NB, 1], I32)
        span_row = sb("span_row", [1, NB, 2], I32)
        ones_row = sb("ones_row", [1, NB])
        win_f = sb("win_f", [1, NB])
        win_sum = sb("win_sum", [1, NB + 1])
        win_first = sb("win_first", [1, NB + 1], I32)
        lo_i = sb("lo_i", [P, NB, 2], I32)
        lo_f = sb("lo_f", [P, NB])
        col_i = sb("col_i", [P, P], I32)
        col_f = sb("col_f", [P, P])
        ident = sb("ident", [P, P])
        sumS = sb("sumS", [P, ZW])
        sumT = sb("sumT", [P, 3, P])
        W0 = sb("W0", [P, 3, F + 1])
        A1 = sb("A1", [P, ROWS1])
        gate_w = sb("gate_w", [ROWS1, GC])
        bias_b = sb("bias_b", [R, F])
        h = sb("h", [R, C, 2 * F])
        ya, yb = (z_mem[1][0:R, k * C * F:(k + 1) * C * F].rearrange("r (c f) -> r c f", f=F) for k in range(2))
        rz = z_mem[1][0:R, 2 * C * F:4 * C * F].rearrange("r (c f) -> r c f", f=2 * F)
        st = [sb(f"st{k}", [R, C]) for k in range(4)]
        eps = sb("eps", [R, 1])

        psM = ps("psM", [P, PB])
        psT = ps("psT", [P, PB])
        psR = ps("psR", [P, PB])
        psN = ps("psN", [P, 5, PB])

        s_w = sem("s_w")
        s_w0z = sem("s_w0z")
        s_const = sem("s_const")
        s_colf = sem("s_colf")
        s_dr = sem("s_dr")
        s_v = sem("s_v")
        s_span = sem("s_span")
        s_var = sem("s_var")
        s_spd = sem("s_spd")
        s_spr = sem("s_spr")
        s_meta = sem("s_meta")
        s_init = sem("s_init")
        s_agg = [sem(f"s_agg{k}") for k in range(2)]
        s_nt = sem("s_nt")
        s_nv = sem("s_nv")
        s_a = sem("s_a")
        s_h = sem("s_h")
        s_hd = sem("s_hd")
        s_ht = sem("s_ht")
        s_hc = sem("s_hc")
        s_g = sem("s_g")
        s_sig = sem("s_sig")
        s_gn = sem("s_gn")
        s_out = sem("s_out")
        s_tab = [sem(f"s_tab{k}") for k in range(2)]
        s_split = sem("s_split")
        s_loads = sem("s_loads")
        s_turn = sem("s_turn")
        s_done = sem("s_done")
        L = []
        for k in range(2):
            L.append(dict(
                inp=[sem(f"l{k}_in{b}") for b in range(2)],
                srcb=[sem(f"l{k}_srcb{b}") for b in range(2)],
                got=[[sem(f"l{k}_got{b}_{j}") for j in range(NCH - 1)] for b in range(2)],
                picked=sem(f"l{k}_picked"), mod=sem(f"l{k}_mod"), pick=sem(f"l{k}_pick"), cand=sem(f"l{k}_cand"),
                grp=sem(f"l{k}_grp"), hot_g=sem(f"l{k}_hot_g"), mask=sem(f"l{k}_mask"), sel=sem(f"l{k}_sel"),
                z=sem(f"l{k}_z"), x=sem(f"l{k}_x"), hot=sem(f"l{k}_hot"), rel=sem(f"l{k}_rel"),
                match=sem(f"l{k}_match"), mm=sem(f"l{k}_mm"), mS=sem(f"l{k}_mS"),
                tp=sem(f"l{k}_tp"), tS=sem(f"l{k}_tS"), res=sem(f"l{k}_res"), acc=sem(f"l{k}_acc")))
        CREDIT = 2 * NCH

        def cols(t, c):
            return t[:, c:N:C]

        def for_each_block(eng, body, peeled=1):
            n = (NB - peeled) // 2
            with eng.Fori(0, n) as i:
                for b in range(2):
                    body(2 * i + b, b, i)
            for b in range(2 * n, NB):
                body(b, b % 2, b // 2)

        def windows_of(eng, b):
            n_win = eng.value_load(span_row[0:1, bass.ds(b, 1), 1:2].rearrange("p a b -> p (a b)"),
                                   min_val=1, max_val=(N - 1) // P + 1)
            first = eng.value_load(win_first[0:1, bass.ds(b, 1)], min_val=0, max_val=NB * P)
            return first, n_win

        def windows_in_all(eng):
            return eng.value_load(win_first[0:1, NB:NB + 1], min_val=1, max_val=NB * P)

        def for_each_window(eng, first, n_win, body):
            with eng.Fori(0, n_win) as q:
                body(first + q, q)

        block = ctx.enter_context(nc.Block())

        @block.sync
        def _(sp):
            def split(k, b, a, t, s):
                gp, e0 = G - H_PE[k], b * BLK
                pat = "(p g) -> p g" if len(a.shape) == 1 else "(p g) f -> p g f"
                sp.dma_start(t[:, 0:gp], a[bass.ds(e0, P * gp)].rearrange(pat, p=P)).then_inc(s, 16)
                sp.dma_start(t[:, gp:G], a[bass.ds(e0 + P * gp, P * H_PE[k])].rearrange(pat, p=P)).then_inc(s, 16)

            def load(k, b, buf):
                s = L[k]["inp"][buf]
                split(k, b, src, idx[buf], s)
                split(k, b, dst, dstb[buf], s)
                split(k, b, *((ea, eab[buf]) if k == 0 else (etype, typ[buf])), s)

            def load_srcb(k, b, buf):
                n = P * H_PE[k]
                sp.dma_start(srcb[buf][:, 0:n], src[bass.ds(b * BLK + BLK - n, n)].partition_broadcast(P)).then_inc(
                    L[k]["srcb"][buf], 16)

            def first_loads(k):
                load(k, 0, 0)
                load_srcb(k, 0, 0)
                load(k, 1, 1)
                load_srcb(k, 1, 1)

            def load_table(k, rows):
                whole = N // (TC * P)
                for c in range(TC):
                    sp.dma_start(table[:, c, 0:whole, :],
                                 rows[0:whole * TC * P, :].rearrange("(g c p) f -> p c g f", c=TC, p=P)[:, c]).then_inc(s_tab[k], 16)
                n0, c = whole * TC * P, 0
                while n0 < N:
                    m = min(P, N - n0)
                    sp.dma_start(table[0:m, c, whole, :], rows[n0:n0 + m, :]).then_inc(s_tab[k], 16)
                    n0, c = n0 + m, c + 1

            def edge_loads(k):
                l = L[k]
                sp.wait_ge(l["mod"], 1)
                load_srcb(k, 2, 0)

                def more(b, buf, with_srcb):
                    sp.wait_ge(l["z"], CREDIT + NCH * (b + 1))
                    sp.sem_inc(s_loads)
                    load(k, b + 2, buf)
                    if with_srcb:
                        load_srcb(k, b + 3, 1 - buf)

                with sp.Fori(0, (NB - 3) // 2) as i:
                    for buf in range(2):
                        more(2 * i + buf, buf, True)
                more(NB - 3, 0, False)

            first_loads(0)
            rows = dst.rearrange("(b e) -> b e", e=BLK)
            nb16 = NB // 16 * 16
            sp.dma_start(dst_rows[0:nb16, :], rows[0:nb16, :]).then_inc(s_dr, 16)
            sp.dma_start(dst_rows[nb16:NB, :], rows[nb16:NB, :]).then_inc(s_dr, 16)
            sp.wait_ge(s_init, 1)
            load_table(0, x)
            sp.wait_ge(s_span, 1)
            sp.dma_start(span_dram, span[:]).then_inc(s_spd, 16)
            sp.wait_ge(s_spd, 16)
            sp.dma_start(span_row[:], span_dram.rearrange("(a b) c -> a b c", a=1)).then_inc(s_spr, 16)
            sp.dma_start(lo_i[:], span_dram.partition_broadcast(P)).then_inc(s_spr, 16)
            sp.wait_ge(s_w0z, 1)
            sp.dma_start(W0[:, 0, 0:F], W_e[0:P, :]).then_inc(s_w, 16)
            sp.dma_start(W0[:, 1, 0:F], W_e[P:2 * P, :]).then_inc(s_w, 16)
            sp.dma_start(W0[1:1 + F, 2, 0:F], b_e).then_inc(s_w, 16)
            sp.dma_start(A1[:, AGG1:ROWS1], A_t).then_inc(s_w, 16)
            sp.dma_start(gate_w[0:F, 0:2 * F], w_hhT[:, 0:2 * F]).then_inc(s_w, 16)
            sp.dma_start(gate_w[0:F, 3 * F:GC], w_hhT[:, 2 * F:3 * F]).then_inc(s_w, 16)
            sp.dma_start(gate_w[F:F + 1, 0:3 * F], b_ih).then_inc(s_w, 16)
            sp.dma_start(gate_w[F + 1:F + 2, 0:2 * F], b_hh[:, 0:2 * F]).then_inc(s_w, 16)
            sp.dma_start(gate_w[F + 1:F + 2, 3 * F:GC], b_hh[:, 2 * F:3 * F]).then_inc(s_w, 16)
            sp.dma_start(gate_w[AGG1:ROWS1, 0:3 * F], w_ihT).then_inc(s_w, 16)
            sp.dma_start(bias_b[:], bias[0, :].partition_broadcast(R)).then_inc(s_w, 16)
            sp.dma_start(h[:, :, 0:F], x.rearrange("(r c) f -> r c f", c=C)).then_inc(s_w, 16)
            edge_loads(0)
            sp.wait_ge(s_h, 1)
            sp.dma_start(h_dram.rearrange("(r c) f -> r c f", c=C), h[:, :, 0:F]).then_inc(s_hd, 16)
            first_loads(1)
            sp.wait_ge(s_hd, 16)
            load_table(1, h_dram)
            edge_loads(1)
            sp.wait_ge(s_out, 1)
            sp.dma_start(out.rearrange("(r c) f -> r c f", c=C), yb[:]).then_inc(s_done, 16)
            sp.wait_ge(s_done, 16)
        N_TAB = 16 * (TC + -(-(N % (TC * P)) // P))
        N_W = 12 * 16

        @block.gpsimd
        def _(pool):
            def gathers(k, table):
                l = L[k]

                cut = chunk_cols(k)

                def body(b, buf, r):
                    pool.wait_ge(l["inp"][buf], 96 * (r + 1))
                    if k == 0:
                        pool.wait_ge(l["x"], b + 1)
                    for j in range(NCH - 1):
                        pool.wait_ge(l["z"], NCH * b + j + 1)
                        pool.sem_inc(s_turn)
                        for g in range(cut[j], cut[j + 1]):
                            pool.indirect_dma_start(
                                xs[buf][:, g, :], None, table,
                                bass.IndirectOffsetOnAxis(ap=idx[buf][:, g:g + 1], axis=0),
                            ).then_inc(l["got"][buf][j], 16)
                for_each_block(pool, body)

            pool.iota(col_i[:], [[1, P]], base=0, channel_multiplier=0).then_inc(s_const, 1)
            pool.memset(ident[:], 0.0).then_inc(s_const, 1)
            pool.wait_ge(s_const, 2)
            pool.affine_select(out=ident[:], in_=ident[:], compare_op=ALU.not_equal, fill=1.0, base=0,
                               pattern=[[-1, P]], channel_multiplier=1).then_inc(s_const, 1)
            pool.iota(chunk_node_i[:], [[P, TC]], base=0, channel_multiplier=1).then_inc(s_const, 1)
            gathers(0, x)
            pool.wait_ge(s_hd, 16)
            gathers(1, h_dram)

        @block.scalar
        def _(act):
            def evacuate(k):
                l = L[k]

                cut = chunk_cols(k)

                def sums_to_rows(w):
                    act.wait_ge(l["tp"], w + 1)
                    if k == 0:
                        act.copy(sumT[0:F + 1, 2, :], psT[0:F + 1, 2 * P:3 * P]).then_inc(l["tS"], 1)
                        act.copy(sumT[:, 0:2, :].rearrange("p a b -> p (a b)"), psT[:, 0:2 * P]).then_inc(l["tS"], 1)
                    else:
                        act.copy(sumT[:, 0, :], psT[:, 0:P]).then_inc(l["tS"], 2)

                def body(b, buf, r):
                    if k == 0:
                        for j in range(NCH - 1):
                            act.wait_ge(l["got"][buf][j], 16 * (cut[j + 1] - cut[j]) * (r + 1))
                        act.wait_ge(l["sel"], b + 1)
                        act.copy(z[buf][:, :, K2 + 1:ZW], xs[buf][:]).then_inc(l["x"], 1)

                    def window(w, q):
                        sums_to_rows(w)
                        act.wait_ge(l["mm"], w + 2)
                        W = ZW if k == 0 else P
                        act.copy(sumS[:, 0:W], psM[:, 0:W]).then_inc(l["mS"], 1)
                    for_each_window(act, *windows_of(act, b), window)
                for_each_block(act, body)
                sums_to_rows(windows_in_all(act))

            act.sem_inc(L[0]["x"], 2)
            act.wait_ge(s_meta, 1)
            evacuate(0)
            act.wait_ge(s_var, 1)
            act.activation(st[2][:], st[1][:], ACT.Sqrt, bias=eps[:, 0:1], scale=1.0 / F).then_inc(s_a, 1)
            for g in range(C // 4):
                act.wait_ge(s_ht, g + 1)
                v = nodeT[0:2 * F, 0:N].rearrange("f (r c) -> f c r", c=C)[:, 4 * g:4 * g + 4, :]
                act.copy(v, psN[0:2 * F, g % 5, 0:4 * R].rearrange("f (c r) -> f c r", r=R)).then_inc(s_hc, 1)
            evacuate(1)
            for g in range(n_gate):
                c0, c1 = 8 * g, min(8 * g + 8, C)
                act.wait_ge(s_g, g + 1)
                act.activation(rz[:, c0:c1, :],
                               psN[0:R, g % 5, 0:GC * (c1 - c0)].rearrange("r (c k) -> r c k", k=GC)[:, :, 0:2 * F],
                               ACT.Sigmoid).then_inc(s_sig, 1)
                act.wait_ge(s_gn, 2 * g + 2)
                act.activation(ya[:, c0:c1, :], ya[:, c0:c1, :], ACT.Tanh).then_inc(s_a, 1)
            act.wait_ge(s_var, 2)
            act.activation(st[2][:], st[1][:], ACT.Sqrt, bias=eps[:, 0:1], scale=1.0 / F).then_inc(s_a, 1)

        @block.tensor
        def _(pe):
            def sums(k):
                l = L[k]
                W = ZW if k == 0 else P

                H = H_PE[k]

                def pick_rows(b):
                    pe.wait_ge(l["cand"], b + 1)
                    for c in range(TC):
                        pe.wait_ge(l["pick"], TC * b + c + 1)
                        for t in range(H):
                            for part in range(2):
                                mm = pe.matmul(psN[:, t // 2, t % 2 * NG * F:(t % 2 + 1) * NG * F],
                                               pick[:, c, t * P:(t + 1) * P],
                                               table_p[part][:, c * NG * F:(c + 1) * NG * F],
                                               start=(c == 0 and part == 0 and t % 2 == 0),
                                               stop=(c == TC - 1 and part == 1), skip_group_check=True)
                        mm.then_inc(l["picked"], 1)

                def flush_transposes(w):
                    pe.wait_ge(l["mS"], w + 1)
                    if k == 0:
                        for c in range(2):
                            pe.transpose(psT[:, c * P:c * P + P], sumS[:, c * P:c * P + P], ident[:])
                        pe.transpose(psT[0:F + 1, 2 * P:3 * P], sumS[:, K2:ZW], ident[:]).then_inc(l["tp"], 1)
                    else:
                        pe.transpose(psT[:, 0:P], sumS[:, 0:P], ident[:]).then_inc(l["tp"], 1)

                def flush_result(w):
                    pe.wait_ge(l["tS"], 2 * w + 2)
                    pe.wait_ge(l["acc"], w + 2)
                    if k == 0:
                        for c in range(2):
                            pe.matmul(psR[0:F + 1, 0:P], W0[:, c, :], sumT[:, c, :], start=(c == 0), stop=False)
                        pe.matmul(psR[0:F + 1, 0:P], W0[0:F + 1, 2, :], sumT[0:F + 1, 2, :],
                                  start=False, stop=True).then_inc(l["res"], 1)
                    else:
                        pe.matmul(psR[0:ROWS1, 0:P], A1[:], sumT[:, 0, :], start=True, stop=True).then_inc(l["res"], 1)

                def body(b, buf, r):
                    if k == 0:
                        pe.wait_ge(l["x"], b + 3)

                    def window(w, q):
                        flush_transposes(w)
                        pe.wait_ge(l["match"], w + 1)
                        for g in range(G):
                            mm = pe.matmul(psM[:, 0:W], onehot[:, g, :], z[buf][:, g, 0:W],
                                           start=(g == 0), stop=(g == G - 1))
                        mm.then_inc(l["mm"], 1)
                        flush_result(w)
                    for_each_window(pe, *windows_of(pe, b), window)
                    if not (isinstance(b, int) and b + 2 >= NB):
                        pick_rows(b + 2)

                pe.wait_ge(s_split, k + 1)
                pick_rows(0)
                pick_rows(1)
                for_each_block(pe, body, peeled=3)
                w = windows_in_all(pe)
                flush_transposes(w)
                flush_result(w)

            pe.wait_ge(s_const, 3)
            pe.wait_ge(s_w, N_W)
            pe.wait_ge(s_meta, 1)
            sums(0)
            pe.wait_ge(s_agg[0], 1)
            for g in range(5):
                for c in range(20 * g, 20 * g + 20):
                    t = pe.transpose(psN[0:R, g, (c - 20 * g) * (F + 1):(c - 20 * g + 1) * (F + 1)],
                                     cols(nodeT[0:F + 1, :], c), ident[0:F + 1, 0:F + 1])
                t.then_inc(s_nt, 1)
            pe.wait_ge(s_h, 1)
            for g in range(C // 4):
                if g >= 5:
                    pe.wait_ge(s_hc, g - 4)
                for c in range(4 * g, 4 * g + 4):
                    t = pe.transpose(psN[0:2 * F, g % 5, (c - 4 * g) * R:(c - 4 * g + 1) * R],
                                     h[:, c, :], ident[0:R, 0:R])
                t.then_inc(s_ht, 1)
            pe.wait_ge(s_hc, C // 4)
            sums(1)
            pe.wait_ge(s_agg[1], 1)
            for g in range(n_gate):
                if g >= 5:
                    pe.wait_ge(s_sig, g - 4)
                    pe.wait_ge(s_gn, 2 * (g - 4))
                for c in range(8 * g, min(8 * g + 8, C)):
                    t = pe.matmul(psN[0:R, g % 5, (c - 8 * g) * GC:(c - 8 * g + 1) * GC],
                                  cols(nodeT, c), gate_w[:], start=True, stop=True)
                t.then_inc(s_g, 1)

        @block.vector
        def _(dve):
            steps = [0]

            def step(ins):
                steps[0] += 1
                ins.then_inc(s_v, 1)
                dve.wait_ge(s_v, steps[0])

            def bc(t, n):
                return t.unsqueeze(2).to_broadcast([t.shape[0], t.shape[1], n])

            def aggregate(k):
                l = L[k]
                p0, p1 = (0, F + 1) if k == 0 else (AGG1, ROWS1)
                H, cut = H_PE[k], chunk_cols(k)
                gp = G - H
                at1, at2 = (dve.alloc_register(f"window_at{k}_{j}") for j in range(2))
                dve.reg_mov(at1, 0)
                dve.reg_mov(at2, 0)

                def add_window(w, at):
                    dve.wait_ge(l["res"], w + 1)
                    dve.wait_ge(l["acc"], w + 1)
                    v = nodeT[p0:p1, bass.ds(dve.snap(at, min_val=0, max_val=N - 1), P)]
                    return dve.tensor_tensor(v, v, psR[p0:p1, 0:P], ALU.add).then_inc(l["acc"], 1)

                def source_mod(b, buf, r):
                    dve.wait_ge(l["srcb"][buf], 16 * (r + 1))
                    dve.tensor_scalar(src_mod[:, 0:H * P].rearrange("q (t p) -> q t p", t=H),
                                      srcb[buf][:, 0:H * P].rearrange("q (p t) -> q t p", t=H), TC * P - 1, None,
                                      ALU.bitwise_and).then_inc(l["mod"], 1)
                    dve.wait_ge(l["mod"], b + 1)

                def pick_columns(b):
                    for c in range(TC):
                        dve.wait_ge(l["picked"], TC * b + c + 1)
                        dve.tensor_scalar(pick[:, c, 0:H * P], src_mod[:, 0:H * P],
                                          chunk_node[:, c:c + 1], None,
                                          ALU.is_equal).then_inc(l["pick"], 1)

                def select_rows(b, buf, r):
                    dve.wait_ge(l["inp"][buf], 96 * (r + 1))
                    dve.tensor_scalar(grp[:, 0:H], idx[buf][:, gp:G], LOG_P + 3, None,
                                      ALU.arith_shift_right).then_inc(l["grp"], 1)
                    dve.wait_ge(l["grp"], b + 1)
                    dve.tensor_tensor(grp_hot[:, 0:H, :], col_f[:, 0:NG].unsqueeze(1).to_broadcast([P, H, NG]),
                                      bc(grp[:, 0:H], NG), ALU.is_equal).then_inc(l["hot_g"], 1)
                    dve.wait_ge(l["hot_g"], b + 1)
                    dve.wait_ge(l["picked"], TC * (b + 2))
                    for t0, t1 in ((0, H // 2 * 2), (H // 2 * 2, H)):
                        if t1 > t0:
                            nbank, m = -(-(t1 - t0) // 2), min(t1 - t0, 2) * NG
                            last = dve.tensor_tensor(
                                cand[:, t0:t1].rearrange("p t g f -> p (t g) f").rearrange("p (k m) f -> p k m f", m=m),
                                psN[:, t0 // 2:t0 // 2 + nbank, 0:m * F].rearrange("p k (m f) -> p k m f", f=F),
                                grp_hot[:, t0:t1].rearrange("p t g -> p (t g)").rearrange("p (k m) -> p k m", m=m)
                                .unsqueeze(3).to_broadcast([P, nbank, m, F]), ALU.mult)
                    last.then_inc(l["cand"], 1)
                    dve.wait_ge(l["cand"], b + 2)
                    if k == 0:
                        dve.wait_ge(l["x"], b + 1)
                    dve.tensor_reduce(xs[buf][:, gp:G, :], cand[:, 0:H].rearrange("p t g f -> p t f g"),
                                      AX.X, ALU.add).then_inc(l["sel"], 1)

                def body(b, buf, r):
                    first, n_win = windows_of(dve, b)
                    dve.wait_ge(l["inp"][buf], 96 * (r + 1))
                    dve.wait_ge(l["rel"], b + first + 1)
                    dve.tensor_scalar(rel[:], dstb[buf][:], lo_f[:, bass.ds(b, 1)], None, ALU.subtract).then_inc(l["rel"], 1)
                    if k == 1:
                        dve.tensor_tensor(typ_hot[:], col_f[:, 0:T].unsqueeze(1).to_broadcast([P, G, T]),
                                          bc(typ[buf], T), ALU.is_equal).then_inc(l["hot"], 1)
                        dve.wait_ge(l["hot"], b + 1)
                    coef, n = (eab[buf], F) if k == 0 else (typ_hot, T)
                    for j in range(NCH):
                        g, m = slice(cut[j], cut[j + 1]), cut[j + 1] - cut[j]
                        if j < NCH - 1:
                            dve.wait_ge(l["got"][buf][j], 16 * m * (r + 1))
                        else:
                            dve.wait_ge(l["sel"], b + 1)
                        dve.tensor_tensor(
                            z[buf][:, g, 0:n * F].rearrange("p g (k i) -> p g k i", i=F),
                            coef[:, g, :].unsqueeze(3).to_broadcast([P, m, n, F]),
                            xs[buf][:, g, :].unsqueeze(2).to_broadcast([P, m, n, F]), ALU.mult).then_inc(l["z"], 1)
                    lo = dve.value_load(span_row[0:1, bass.ds(b, 1), 0:1].rearrange("p a b -> p (a b)"),
                                        min_val=0, max_val=N - 1)

                    def window(w, q):
                        dve.wait_ge(l["mm"], w + 1)
                        dve.wait_ge(l["rel"], b + w + 2)
                        dve.tensor_tensor(onehot[:], col_f[:].unsqueeze(1).to_broadcast([P, G, P]),
                                          bc(rel, P), ALU.is_equal).then_inc(l["match"], 1)
                        dve.wait_ge(l["match"], w + 1)
                        dve.tensor_scalar(rel[:], rel[:], float(P), None, ALU.subtract).then_inc(l["rel"], 1)
                        add_window(w, at2)
                        dve.reg_mov(at2, dve.snap(at1, min_val=0, max_val=N - 1))
                        dve.reg_mov(at1, lo + q * P)
                    for_each_window(dve, first, n_win, window)
                    more = not (isinstance(b, int) and b + 2 >= NB)
                    if more:
                        source_mod(b + 2, buf, r + 1)
                        pick_columns(b + 2)
                    if not (isinstance(b, int) and b + 1 >= NB):
                        select_rows(b + 1, 1 - buf, r + buf)

                dve.wait_ge(s_tab[k], N_TAB)
                rows = table[:].rearrange("p c g f -> p (c g f)")
                step(dve.tensor_copy(table_p[0][:], rows))
                step(dve.tensor_tensor(table_p[1][:], rows, table_p[0][:], ALU.subtract))
                dve.sem_inc(s_split, 1)
                if k == 0:
                    for b in range(2):
                        step(dve.memset(z[b][:, :, K2:K2 + 1], 1.0))
                    dve.sem_inc(s_meta, 1)
                for b in range(2):
                    source_mod(b, b, 0)
                    pick_columns(b)
                    if b == 0:
                        select_rows(0, 0, 0)
                for_each_block(dve, body, peeled=3)
                last = windows_in_all(dve)
                add_window(last, at2)
                add_window(last + 1, at1)
                dve.wait_ge(l["acc"], last + 3)
                dve.sem_inc(s_agg[k], 1)

            def centre_and_square():
                step(dve.tensor_reduce(st[0][:], ya[:], AX.X, ALU.add))
                step(dve.tensor_scalar(st[0][:], st[0][:], 1.0 / F, None, ALU.mult))
                step(dve.tensor_tensor(yb[:], ya[:], bc(st[0], F), ALU.subtract))
                step(dve.tensor_tensor(ya[:], yb[:], yb[:], ALU.mult))
                step(dve.tensor_reduce(st[1][:], ya[:], AX.X, ALU.add))
                dve.sem_inc(s_var, 1)

            for l in L:
                dve.sem_inc(l["z"], CREDIT)
                dve.sem_inc(l["picked"], TC)
                dve.sem_inc(l["cand"], 1)
                dve.sem_inc(l["mm"], 1)
                dve.sem_inc(l["acc"], 1)
                dve.sem_inc(l["rel"], 1)
            step(dve.memset(table[:], 0.0))
            dve.sem_inc(s_init, 1)
            step(dve.memset(W0[:], 0.0))
            step(dve.memset(W0[0:1, 2, F:F + 1], 1.0))
            dve.memset(A1[:], 0.0)
            step(dve.memset(gate_w[:], 0.0))
            step(dve.memset(h[:], 0.0))
            dve.sem_inc(s_w0z, 1)
            dve.memset(ones_row[:], 1.0)
            dve.memset(win_sum[:], 0.0)
            dve.memset(eps[:], 1e-5)
            dve.memset(nodeT[:], 0.0)
            step(dve.memset(sumS[:], 0.0))
            step(dve.memset(psR[:], 0.0))
            step(dve.memset(h[:, :, F:F + 2], 1.0))
            dve.wait_ge(s_const, 1)
            step(dve.tensor_copy(col_f[:], col_i[:]))
            dve.wait_ge(s_const, 4)
            step(dve.tensor_copy(chunk_node[:], chunk_node_i[:]))
            dve.wait_ge(s_dr, 32)
            step(dve.tensor_reduce(span[:, 0:1], dst_rows[:], AX.X, ALU.min))
            step(dve.tensor_reduce(span_hi[:], dst_rows[:], AX.X, ALU.max))
            step(dve.tensor_tensor(span_hi[:], span_hi[:], span[:, 0:1], ALU.subtract))
            step(dve.tensor_scalar(span_hi[:], span_hi[:], LOG_P, None, ALU.arith_shift_right))
            step(dve.tensor_scalar(span[:, 1:2], span_hi[:], 1.0, None, ALU.add))
            dve.sem_inc(s_span, 1)
            dve.wait_ge(s_spr, 32)
            step(dve.tensor_copy(win_f[:], span_row[0:1, :, 1]))
            step(dve.tensor_copy(lo_f[:], lo_i[:, :, 0]))
            step(dve.tensor_tensor_scan(win_sum[:, 1:NB + 1], ones_row[:], win_f[:], 0.0, ALU.mult, ALU.add))
            step(dve.tensor_copy(win_first[:], win_sum[:]))
            dve.sem_inc(L[0]["res"], 1)
            dve.sem_inc(L[0]["mS"], 1)

            aggregate(0)

            dve.wait_ge(s_w, N_W)
            step(dve.tensor_tensor(h[:, :, 0:F], h[:, :, 0:F], bias_b[:].unsqueeze(1).to_broadcast([R, C, F]), ALU.add))
            for g in range(5):
                dve.wait_ge(s_nt, g + 1)
                v = psN[0:R, g, 0:20 * (F + 1)].rearrange("r (c f) -> r c f", f=F + 1)
                cs = slice(20 * g, 20 * g + 20)
                step(dve.tensor_scalar(st[0][:, cs], v[:, :, F], 1.0, None, ALU.max))
                step(dve.reciprocal(st[0][:, cs], st[0][:, cs]))
                step(dve.tensor_tensor(ya[:, cs, :], v[:, :, 0:F], bc(st[0][:, cs], F), ALU.mult))
            step(dve.tensor_tensor(ya[:], ya[:], h[:, :, 0:F], ALU.add))
            centre_and_square()
            dve.wait_ge(s_a, 1)
            step(dve.reciprocal(st[3][:], st[2][:]))
            dve.tensor_tensor(h[:, :, 0:F], yb[:], bc(st[3], F), ALU.mult).then_inc(s_h, 1)
            step(dve.memset(sumS[:], 0.0))
            step(dve.memset(psR[:], 0.0))
            dve.sem_inc(L[1]["res"], 1)
            dve.sem_inc(L[1]["mS"], 1)

            aggregate(1)

            for g in range(n_gate):
                c0, c1 = 8 * g, min(8 * g + 8, C)
                v = psN[0:R, g % 5, 0:GC * (c1 - c0)].rearrange("r (c k) -> r c k", k=GC)
                dve.wait_ge(s_sig, g + 1)
                dve.tensor_tensor(ya[:, c0:c1, :], rz[:, c0:c1, 0:F], v[:, :, 3 * F:GC], ALU.mult).then_inc(s_gn, 1)
                dve.wait_ge(s_gn, 2 * g + 1)
                dve.tensor_tensor(ya[:, c0:c1, :], ya[:, c0:c1, :], v[:, :, 2 * F:3 * F], ALU.add).then_inc(s_gn, 1)
            dve.wait_ge(s_a, 1 + n_gate)
            hv = h[:, :, 0:F]
            step(dve.tensor_tensor(yb[:], hv, ya[:], ALU.subtract))
            step(dve.tensor_tensor(yb[:], yb[:], rz[:, :, F:2 * F], ALU.mult))
            step(dve.tensor_tensor(ya[:], ya[:], hv, ALU.add))
            step(dve.tensor_tensor(ya[:], ya[:], yb[:], ALU.add))
            centre_and_square()
            dve.wait_ge(s_a, 2 + n_gate)
            step(dve.reciprocal(st[3][:], st[2][:]))
            dve.tensor_tensor(yb[:], yb[:], bc(st[3], F), ALU.mult).then_inc(s_out, 1)


_INS = ["x", "src", "dst", "edge_attr_16", "edge_type_8", "W_e", "b_e", "bias", "A_t", "w_ihT", "w_hhT", "b_ih", "b_hh"]


def kernel(x, src, dst, edge_attr_16, edge_type_8, L0_gnn_W_e, L0_gnn_b_e, L0_gnn_bias, L1_gnn_edge_emb,
           L1_gnn_w_ih, L1_gnn_w_hh, L1_gnn_b_ih, L1_gnn_b_hh):
    import numpy as np
    import concourse.bacc as bacc
    from concourse.bass_utils import run_bass_kernel_spmd

    n_types = L1_gnn_edge_emb.shape[0]
    given = dict(
        x=x, src=src, dst=dst, edge_attr_16=edge_attr_16, edge_type_8=edge_type_8,
        W_e=np.asarray(L0_gnn_W_e).reshape(K2, F), b_e=np.asarray(L0_gnn_b_e).reshape(F, F),
        bias=np.asarray(L0_gnn_bias).reshape(1, F),
        A_t=np.asarray(L1_gnn_edge_emb).reshape(n_types, F, F).transpose(0, 2, 1).reshape(n_types * F, F),
        w_ihT=np.asarray(L1_gnn_w_ih).T, w_hhT=np.asarray(L1_gnn_w_hh).T,
        b_ih=np.asarray(L1_gnn_b_ih).reshape(1, 3 * F), b_hh=np.asarray(L1_gnn_b_hh).reshape(1, 3 * F))
    nc = bacc.Bacc("TRN2", target_bir_lowering=False, num_devices=1)
    arrays, args = {}, []
    for name in _INS:
        a = np.ascontiguousarray(given[name])
        arrays[f"in_{name}"] = a
        args.append(nc.dram_tensor(f"in_{name}", a.shape, mybir.dt.from_np(a.dtype), kind="ExternalInput").ap())
    args.append(nc.dram_tensor("out_0", x.shape, F32, kind="ExternalOutput").ap())
    build(nc, *args)
    r = run_bass_kernel_spmd(nc, [arrays], core_ids=[0])
    return r.results[0]["out_0"]
```

```python
import concourse.bass as bass
from concourse import mybir

P = 128
F = 16
K2 = F * F
ALU = mybir.AluOpType
ACT = mybir.ActivationFunctionType
AX = mybir.AxisListType
F32 = mybir.dt.float32
F32R = mybir.dt.float32r
I32 = mybir.dt.int32
U16 = mybir.dt.uint16

G = 25
H_PE = (6, 8)
NCH = 5
TC = 7
TC_ACT = 3
TC_DVE = TC - TC_ACT
GRP = TC * P
DIV_MUL, DIV_SHIFT = 9363, 16
assert all(q * DIV_MUL >> DIV_SHIFT == q // TC for q in range(P)) and P * DIV_MUL < 2 ** 24
BLK = P * G
LOG_P = 7


SPLIT = ((NCH - 1, 0), (NCH - 1,))
SPLIT_COLS = (H_PE[0] + 2, H_PE[1])
ORDER = [NCH - 1] + list(range(NCH - 1))


def chunk_cols(k):
    gp = G - H_PE[k]
    if k == 1:
        return [gp * j // (NCH - 1) for j in range(NCH)] + [G]
    n0 = SPLIT_COLS[0] - H_PE[0]
    return [0] + [n0 + (gp - n0) * j // (NCH - 2) for j in range(NCH - 1)] + [G]


def build(nc, x, src, dst, ea, etype, W_e, b_e, bias, A_t, w_ihT, w_hhT, b_ih, b_hh, out):
    N, E = x.shape[0], src.shape[0]
    T = A_t.shape[0] // F
    NB = E // BLK
    assert NB * BLK == E and NB % 2 == 1 and NB <= P and T * F == P
    R = 125
    C = N // R
    assert R * C == N
    ZW = K2 + 1 + F
    ZS = ZW + 1
    NPAD = N + P
    AGG1 = 32
    ROWS1 = AGG1 + F
    NG = -(-N // GRP)
    HM = max(H_PE)
    GB = 5
    GS, GW = 96, P
    n_gate = C // (2 * GB)
    assert (GB - 1) * GS + GW <= 512 and n_gate * 2 * GB == C
    GC = 4 * F
    PB = 512

    h_dram = nc.dram_tensor("h_rows", [N, F], F32, kind="Internal").ap()
    span_dram = nc.dram_tensor("block_span", [NB, 2], I32, kind="Internal").ap()

    mod_dram = [nc.dram_tensor(f"src_mod_l{k}", [NB, P * H_PE[k]], U16, kind="Internal").ap() for k in range(2)]
    grp_dram = nc.dram_tensor("src_grp", [NB, P * max(H_PE)], I32, kind="Internal").ap()

    from contextlib import ExitStack
    with ExitStack() as ctx:
        def sb(name, shape, dt=F32):
            return ctx.enter_context(nc.sbuf_tensor(name, shape, dt))[tuple(slice(None) for _ in shape)]

        def ps(name, shape):
            return ctx.enter_context(nc.psum_tensor(name, shape, F32))[tuple(slice(None) for _ in shape)]

        def sem(name):
            return ctx.enter_context(nc.semaphore(name))

        nodeT = sb("nodeT", [ROWS1, NPAD])
        z_mem = [sb(f"z{b}", [P, G * ZS]) for b in range(2)]
        z = [[m[:, 0:G * w].rearrange("p (g c) -> p g c", c=w) for m in z_mem] for w in (ZS, P)]
        onehot_r = sb("onehot", [P, G, P], F32R)
        onehot = onehot_r.bitcast(F32)
        src_mod = [sb(f"src_mod{b}", [P, HM * P], U16) for b in range(2)]
        dist = sb("dist", [P, HM * P])
        part0, part1 = SPLIT_COLS[0] * ZS, SPLIT_COLS[1] * P
        pick0 = TC * H_PE[0] * P
        pick_mem = sb("pick", [P, max(TC * HM * P, pick0 + part0)], F32R)
        pick = [pick_mem[:, 0:TC * H * P].rearrange("p (c n) -> p c n", c=TC) for H in H_PE]
        split_mem = sb("split", [P, max(2 * part1, part0)], F32R)
        z_part = [[m.rearrange("p (g c) -> p g c", c=ZS) for m in (pick_mem[:, pick0:pick0 + part0], split_mem[:, 0:part0])],
                  [split_mem[:, 0:2 * part1].rearrange("p (g n c) -> p g n c", n=2, c=P)[:, :, n, :] for n in range(2)]]
        z_both = split_mem[:, 0:2 * part1].rearrange("p (g c) -> p g c", c=2 * P)
        chunk_node_i = sb("chunk_node_i", [P, TC], I32)
        chunk_node = sb("chunk_node", [P, TC])
        table_p = [sb(f"table_{n}", [P, TC * NG * F], F32R) for n in ("hi", "lo")]
        neg_node = sb("neg_node", [P, TC])
        one = sb("one", [P, 1])
        zero = sb("zero", [P, 1])
        grp = [sb(f"grp{b}", [P, HM], I32) for b in range(2)]
        grp_hot = [sb(f"grp_hot{b}", [P, HM, NG]) for b in range(2)]
        cand1 = z_mem[0][:, BLK + TC * NG * F:BLK + (TC + H_PE[1]) * NG * F]
        cand = [sb("cand", [P, H_PE[0], NG, F]), cand1.rearrange("p (t g f) -> p t g f", g=NG, f=F)]
        xh = H_PE[1] * F
        x_hi, x_lo = (z_mem[1][:, BLK + n * xh:BLK + (n + 1) * xh].rearrange("p (g f) -> p g f", f=F) for n in range(2))
        x_hi, x_lo = x_hi.bitcast(F32R), x_lo.bitcast(F32R)
        typ_hot = z_mem[1][:, BLK + 2 * xh:BLK + 2 * xh + G * T].rearrange("p (g t) -> p g t", t=T)
        xs = [sb(f"xs{b}", [P, G, F]) for b in range(2)]
        idx = [sb(f"idx{b}", [P, G], I32) for b in range(2)]
        dstb = [sb(f"dstb{b}", [P, G], I32) for b in range(2)]
        eab = [sb(f"eab{b}", [P, G, F]) for b in range(2)]
        typ = [sb(f"typ{b}", [P, G], I32) for b in range(2)]
        rel = sb("rel", [P, G])
        t0, t1 = BLK, BLK + TC * NG * F
        table = z_mem[0][:, t0:t1].rearrange("p (c g f) -> p c g f", c=TC, f=F)
        dst_rows = z_mem[0][0:NB, 0:BLK].bitcast(I32)
        n_src = P * HM
        src_rows, src_q, src_g, src_v = (z_mem[1][0:NB, n * n_src:(n + 1) * n_src].bitcast(I32) for n in range(4))
        src_out = [z_mem[1][0:NB, 4 * n_src + k * n_src // 2:4 * n_src + (k + 1) * n_src // 2].bitcast(U16)
                   [:, 0:P * H_PE[k]] for k in range(2)]
        span = sb("span", [NB, 2], I32)
        span_hi = sb("span_hi", [NB, 1], I32)
        span_row = sb("span_row", [1, NB, 2], I32)
        ones_row = sb("ones_row", [1, NB])
        win_f = sb("win_f", [1, NB])
        win_sum = sb("win_sum", [1, NB + 1])
        win_first = sb("win_first", [1, NB + 1], I32)
        lo_i = z_mem[1][:, 5 * n_src:5 * n_src + 2 * NB].bitcast(I32).rearrange("p (b c) -> p b c", c=2)
        lo_f = sb("lo_f", [P, NB])
        col_i = sb("col_i", [P, P], I32)
        col_f = sb("col_f", [P, P])
        ident = sb("ident", [P, P])
        sumS = sb("sumS", [P, ZW])
        sumT = sb("sumT", [P, 3, P])
        W0 = sb("W0", [P, 3, F + 1])
        A1 = sb("A1", [P, ROWS1])
        gate_w = sb("gate_w", [ROWS1, GW])
        bias_b = sb("bias_b", [R, F])
        h = sb("h", [R, C, F])
        ya, yb = (z_mem[1][0:R, k * C * F:(k + 1) * C * F].rearrange("r (c f) -> r c f", f=F) for k in range(2))
        rz = z_mem[1][0:R, 2 * C * F:4 * C * F].rearrange("r (c f) -> r c f", f=2 * F)
        h_pad = z_mem[1][0:R, 2 * C * F:4 * C * F].rearrange("r (c f) -> r c f", f=2 * F)
        st = [sb(f"st{k}", [R, C]) for k in range(4)]
        eps = sb("eps", [R, 1])

        psM = ps("psM", [P, PB])
        psT = ps("psT", [P, PB])
        psR = ps("psR", [P, PB])
        psN = ps("psN", [P, 5, PB])

        s_w = sem("s_w")
        s_zero = sem("s_zero")
        s_nz = sem("s_nz")
        s_n = sem("s_n")
        s_w0z = sem("s_w0z")
        s_const = sem("s_const")
        s_sr = sem("s_sr")
        s_mod = sem("s_mod")
        s_modd = sem("s_modd")
        s_dr = sem("s_dr")
        s_v = sem("s_v")
        s_span = sem("s_span")
        s_var = sem("s_var")
        s_spd = sem("s_spd")
        s_spr = sem("s_spr")
        s_node = sem("s_node")
        s_meta = sem("s_meta")
        s_init = sem("s_init")
        s_agg = [sem(f"s_agg{k}") for k in range(2)]
        s_nt = sem("s_nt")
        s_a = sem("s_a")
        s_h = sem("s_h")
        s_hs = sem("s_hs")
        s_hd = sem("s_hd")
        s_ht = sem("s_ht")
        s_hc = sem("s_hc")
        s_g = sem("s_g")
        s_sig = sem("s_sig")
        s_gn = sem("s_gn")
        s_out = sem("s_out")
        s_tab = [sem(f"s_tab{k}") for k in range(2)]
        s_split = sem("s_split")
        s_loads = sem("s_loads")
        s_turn = sem("s_turn")
        s_done = sem("s_done")
        L = []
        for k in range(2):
            one_per = dict(
                pick="DVE's one-hot columns for PE's gathers: TC_DVE chunks per block",
                pick_act="ACT's: TC_ACT chunks per block",
                dist="ACT's |difference|s",
                picked="PE used a chunk of one-hot columns: TC per block",
                hot_g="one-hot groups of the PE columns' sources",
                cand="DVE took a block's candidates from psN",
                sel="xs of the PE columns",
                hi="high parts", lo="low parts", zh="high parts of z (layer 1)",
                z="chunks of z made: NCH per block", x="x copied to them (layer 0)",
                hot="one-hot types (layer 1)",
                rel="rel written: once per block and once per window",
                match="one-hot rows of a window", mm="a window's products summed in psM", mS="... copied to sumS",
                tp="... transposed to psT", tS="... copied to sumT: 2 per window",
                res="a window's result in psR", acc="... added to nodeT")
            l = {what: sem(f"l{k}_{what}") for what in one_per}
            l["idx"], l["inp"], l["src"] = ([sem(f"l{k}_{what}{b}") for b in range(2)]
                                            for what in ("idx", "in", "src"))
            l["got"] = [[sem(f"l{k}_got{b}_{j}") for j in range(NCH - 1)] for b in range(2)]
            L.append(l)
        CREDIT = 2 * NCH

        def parts_of(k, j):
            cut = chunk_cols(k)
            at = sum(cut[i + 1] - cut[i] for i in SPLIT[k][:SPLIT[k].index(j)])
            return slice(at, at + cut[j + 1] - cut[j])

        def gates(g):
            j = g % 2 * 2
            return psN[0:R, j:j + 2, 0:GB * GS].rearrange("r j (c k) -> r j c k", k=GS)

        def cols(t, c):
            return t[:, c:N:C]

        def for_each_block(eng, body, peeled=1):
            n = (NB - peeled) // 2
            with eng.Fori(0, n) as i:
                for b in range(2):
                    body(2 * i + b, b, i)
            for b in range(2 * n, NB):
                body(b, b % 2, b // 2)

        def windows_of(eng, b):
            n_win = eng.value_load(span_row[0:1, bass.ds(b, 1), 1:2].rearrange("p a b -> p (a b)"),
                                   min_val=1, max_val=(N - 1) // P + 1)
            first = eng.value_load(win_first[0:1, bass.ds(b, 1)], min_val=0, max_val=NB * P)
            return first, n_win

        def windows_in_all(eng):
            return eng.value_load(win_first[0:1, NB:NB + 1], min_val=1, max_val=NB * P)

        def for_each_window(eng, first, n_win, body):
            with eng.Fori(0, n_win) as q:
                body(first + q, q)

        block = ctx.enter_context(nc.Block())

        @block.sync
        def _(sp):
            def split(k, b, a, t, s):
                gp, e0 = G - H_PE[k], b * BLK
                pat = "(p g) -> p g" if len(a.shape) == 1 else "(p g) f -> p g f"
                sp.dma_start(t[:, 0:gp], a[bass.ds(e0, P * gp)].rearrange(pat, p=P)).then_inc(s, 16)
                sp.dma_start(t[:, gp:G], a[bass.ds(e0 + P * gp, P * H_PE[k])].rearrange(pat, p=P)).then_inc(s, 16)

            n16 = R // 16 * 16

            def node_rows(out_t, in_t, s):
                for a, b in ((0, n16), (n16, R)):
                    sp.dma_start(out_t[a:b], in_t[a:b]).then_inc(s, 16)

            def load_idx(k, b, buf):
                gp = G - H_PE[k]
                sp.dma_start(idx[buf][:, 0:gp], src[bass.ds(b * BLK, P * gp)].rearrange("(p g) -> p g", p=P)).then_inc(L[k]["idx"][buf], 16)

            def load(k, b, buf):
                s = L[k]["inp"][buf]
                split(k, b, dst, dstb[buf], s)
                split(k, b, *((ea, eab[buf]) if k == 0 else (etype, typ[buf])), s)

            def load_src(k, b, buf):
                H, s = H_PE[k], L[k]["src"][buf]
                sp.dma_start(src_mod[buf][:, 0:P * H], mod_dram[k][bass.ds(b, 1), :].rearrange("a n -> (a n)")
                             .partition_broadcast(P)).then_inc(s, 16)
                sp.dma_start(grp[buf][:, 0:H], grp_dram[bass.ds(b, 1), P * (HM - H):P * HM]
                             .rearrange("a (p t) -> (a p) t", p=P)).then_inc(s, 16)

            def load_table(k, rows):
                whole = N // GRP
                for c in range(TC):
                    sp.dma_start(table[:, c, 0:whole, :],
                                 rows[0:whole * GRP, :].rearrange("(g c p) f -> p c g f", c=TC, p=P)[:, c]).then_inc(s_tab[k], 16)
                n0, c = whole * GRP, 0
                while n0 < N:
                    m = min(P, N - n0)
                    sp.dma_start(table[0:m, c, whole, :], rows[n0:n0 + m, :]).then_inc(s_tab[k], 16)
                    n0, c = n0 + m, c + 1

            def edge_loads(k):
                l = L[k]

                def load_src_after(b, buf):
                    sp.wait_ge(l["pick"], TC_DVE * (b - 1))
                    sp.wait_ge(l["pick_act"], TC_ACT * (b - 1) + 1)
                    sp.sem_inc(s_loads)
                    load_src(k, b, buf)

                load_src_after(2, 0)

                cut = chunk_cols(k)

                def more(b, buf, r, with_src):
                    for j in range(NCH - 1):
                        sp.wait_ge(l["got"][buf][j], 16 * (cut[j + 1] - cut[j]) * (r + 1))
                        sp.sem_inc(s_loads)
                    load_idx(k, b + 2, buf)
                    sp.wait_ge(l["z"], CREDIT + NCH * (b + 1))
                    sp.sem_inc(s_loads)
                    load(k, b + 2, buf)
                    if with_src:
                        load_src_after(b + 3, 1 - buf)

                with sp.Fori(0, (NB - 3) // 2) as i:
                    for buf in range(2):
                        more(2 * i + buf, buf, i, True)
                more(NB - 3, 0, (NB - 3) // 2, False)

            load_idx(0, 0, 0)
            load(0, 0, 0)
            sp.dma_start(src_rows, src.rearrange("(b e) -> b e", e=BLK)[:, BLK - n_src:BLK]).then_inc(s_sr, 16)
            load_idx(0, 1, 1)
            load(0, 1, 1)
            rows = dst.rearrange("(b e) -> b e", e=BLK)
            nb16 = NB // 16 * 16
            sp.dma_start(dst_rows[0:nb16, :], rows[0:nb16, :]).then_inc(s_dr, 16)
            sp.dma_start(dst_rows[nb16:NB, :], rows[nb16:NB, :]).then_inc(s_dr, 16)
            sp.wait_ge(s_init, 1)
            load_table(0, x)
            sp.wait_ge(s_mod, 1)
            for k in range(2):
                sp.dma_start(mod_dram[k], src_out[k]).then_inc(s_modd, 16)
            sp.dma_start(grp_dram, src_g).then_inc(s_modd, 16)
            sp.wait_ge(s_modd, 48)
            for b in range(2):
                load_src(0, b, b)
            sp.wait_ge(s_span, 1)
            sp.dma_start(span_dram, span[:]).then_inc(s_spd, 16)
            sp.wait_ge(s_spd, 16)
            sp.dma_start(span_row[:], span_dram.rearrange("(a b) c -> a b c", a=1)).then_inc(s_spr, 16)
            sp.dma_start(lo_i[:], span_dram.partition_broadcast(P)).then_inc(s_spr, 16)
            sp.wait_ge(s_w0z, 1)
            sp.dma_start(W0[:, 0, 0:F], W_e[0:P, :]).then_inc(s_w, 16)
            sp.dma_start(W0[:, 1, 0:F], W_e[P:2 * P, :]).then_inc(s_w, 16)
            sp.dma_start(W0[1:1 + F, 2, 0:F], b_e).then_inc(s_w, 16)
            sp.dma_start(A1[:, AGG1:ROWS1], A_t).then_inc(s_w, 16)
            sp.dma_start(gate_w[0:F, 0:2 * F], w_hhT[:, 0:2 * F]).then_inc(s_w, 16)
            sp.dma_start(gate_w[0:F, 3 * F:GC], w_hhT[:, 2 * F:3 * F]).then_inc(s_w, 16)
            sp.dma_start(gate_w[F:F + 1, 0:3 * F], b_ih).then_inc(s_w, 16)
            sp.dma_start(gate_w[F + 1:F + 2, 0:2 * F], b_hh[:, 0:2 * F]).then_inc(s_w, 16)
            sp.dma_start(gate_w[F + 1:F + 2, 3 * F:GC], b_hh[:, 2 * F:3 * F]).then_inc(s_w, 16)
            sp.dma_start(gate_w[AGG1:ROWS1, 0:3 * F], w_ihT).then_inc(s_w, 16)
            sp.dma_start(bias_b[:], bias[0, :].partition_broadcast(R)).then_inc(s_w, 16)
            node_rows(h[:], x.rearrange("(r c) f -> r c f", c=C), s_w)
            edge_loads(0)
            sp.wait_ge(s_h, 1)
            node_rows(h_dram.rearrange("(r c) f -> r c f", c=C), yb, s_hd)
            for b in range(2):
                load_idx(1, b, b)
                load(1, b, b)
                load_src(1, b, b)
            sp.wait_ge(s_hd, 32)
            load_table(1, h_dram)
            edge_loads(1)
            sp.wait_ge(s_out, 1)
            node_rows(out.rearrange("(r c) f -> r c f", c=C), yb, s_done)
            sp.wait_ge(s_done, 32)
        N_TAB = 16 * (TC + -(-(N % GRP) // P))
        N_W = 13 * 16

        @block.gpsimd
        def _(pool):
            def gathers(k, table):
                l = L[k]

                cut = chunk_cols(k)

                def body(b, buf, r):
                    pool.wait_ge(l["idx"][buf], 16 * (r + 1))
                    for j in range(NCH - 1):
                        n = NCH * b + ORDER.index(j) + 1
                        if k == 0:
                            pool.wait_ge(l["x"], n)
                        pool.wait_ge(l["z"], n)
                        pool.sem_inc(s_turn)
                        for g in range(cut[j], cut[j + 1]):
                            pool.indirect_dma_start(
                                xs[buf][:, g, :], None, table,
                                bass.IndirectOffsetOnAxis(ap=idx[buf][:, g:g + 1], axis=0),
                            ).then_inc(l["got"][buf][j], 16)
                for_each_block(pool, body)

            pool.iota(col_i[:], [[1, P]], base=0, channel_multiplier=0).then_inc(s_const, 1)
            pool.memset(ident[:], 0.0).then_inc(s_const, 1)
            pool.wait_ge(s_const, 2)
            pool.affine_select(out=ident[:], in_=ident[:], compare_op=ALU.not_equal, fill=1.0, base=0,
                               pattern=[[-1, P]], channel_multiplier=1).then_inc(s_const, 1)
            pool.iota(chunk_node_i[:], [[P, TC]], base=0, channel_multiplier=1).then_inc(s_const, 1)
            gathers(0, x)
            pool.wait_ge(s_hd, 32)
            gathers(1, h_dram)

        @block.scalar
        def _(act):
            def evacuate(k):
                l = L[k]

                cut = chunk_cols(k)

                def sums_to_rows(w):
                    act.wait_ge(l["tp"], w + 1)
                    if k == 0:
                        act.copy(sumT[0:F + 1, 2, :], psT[0:F + 1, 2 * P:3 * P]).then_inc(l["tS"], 1)
                        act.copy(sumT[:, 0:2, :].rearrange("p a b -> p (a b)"), psT[:, 0:2 * P]).then_inc(l["tS"], 1)
                    else:
                        act.copy(sumT[:, 0, :], psT[:, 0:P]).then_inc(l["tS"], 2)

                def pick_columns(b, buf, r):
                    n = P * H_PE[k]
                    act.wait_ge(l["src"][buf], 32 * (r + 1))
                    for j in range(TC_ACT):
                        c = TC_DVE + j
                        act.wait_ge(l["pick_act"], TC_ACT * b + j + 1)
                        act.activation(dist[:, 0:n], src_mod[buf][:, 0:n], ACT.Abs, bias=neg_node[:, c:c + 1]).then_inc(l["dist"], 1)
                        act.wait_ge(l["dist"], TC_ACT * b + j + 1)
                        act.wait_ge(l["picked"], TC * b + c + 1)
                        act.activation(pick[k][:, c, 0:n], dist[:, 0:n], ACT.Relu, bias=one[:, 0:1], scale=-1.0).then_inc(l["pick_act"], 1)

                def copy_x(b, buf, r, j):
                    if j == NCH - 1:
                        act.wait_ge(l["sel"], b + 1)
                    else:
                        act.wait_ge(l["got"][buf][j], 16 * (cut[j + 1] - cut[j]) * (r + 1))
                    act.copy(z[0][buf][:, cut[j]:cut[j + 1], K2 + 1:ZW], xs[buf][:, cut[j]:cut[j + 1], :]).then_inc(l["x"], 1)

                def high_part(b, buf, j):
                    if k == 0:
                        n = ORDER.index(j) + 1
                        act.wait_ge(l["z"], CREDIT + NCH * b + n)
                        act.wait_ge(l["x"], CREDIT + NCH * b + n)
                        act.copy(z_part[0][0][:, parts_of(0, j), :], z[0][buf][:, cut[j]:cut[j + 1], :]).then_inc(l["hi"], 1)
                    else:
                        act.wait_ge(l["sel"], b + 1)
                        act.wait_ge(l["z"], CREDIT + NCH * (b - 1) + 1)
                        act.copy(x_hi, xs[buf][:, cut[NCH - 1]:G, :]).then_inc(l["hi"], 1)

                def body(b, buf, r):
                    for j in SPLIT[k]:
                        if k == 0:
                            copy_x(b, buf, r, j)
                        high_part(b, buf, j)
                    if k == 0:
                        copy_x(b, buf, r, ORDER[2])
                    if not (isinstance(b, int) and b + 2 >= NB):
                        pick_columns(b + 2, buf, r + 1)
                    if k == 0:
                        for j in ORDER[3:]:
                            copy_x(b, buf, r, j)

                    def window(w, q):
                        sums_to_rows(w)
                        act.wait_ge(l["mm"], w + 2)
                        W = ZW if k == 0 else 2 * P
                        act.copy(sumS[:, 0:W], psM[:, 0:W]).then_inc(l["mS"], 1)
                    for_each_window(act, *windows_of(act, b), window)
                if k == 1:
                    h_to_rows()
                pick_columns(0, 0, 0)
                pick_columns(1, 1, 0)
                if k == 0:
                    act.wait_ge(s_meta, 1)
                for_each_block(act, body, peeled=3)
                sums_to_rows(windows_in_all(act))

            def h_to_rows():
                for g in range(C // 4):
                    act.wait_ge(s_ht, g + 1)
                    v = nodeT[0:2 * F, 0:N].rearrange("f (r c) -> f c r", c=C)[:, 4 * g:4 * g + 4, :]
                    act.copy(v, psN[0:2 * F, g % 5, 0:4 * R].rearrange("f (c r) -> f c r", r=R)).then_inc(s_hc, 1)

            act.sem_inc(L[0]["x"], CREDIT)
            act.wait_ge(s_zero, 1)
            act.copy(nodeT[:], zero[0:ROWS1, 0:1].to_broadcast([ROWS1, NPAD])).then_inc(s_nz, 1)
            act.wait_ge(s_node, 1)
            evacuate(0)
            act.wait_ge(s_var, 1)
            act.activation(st[2][:], st[1][:], ACT.Sqrt, bias=eps[:, 0:1], scale=1.0 / F).then_inc(s_a, 1)
            evacuate(1)
            for g in range(n_gate):
                cs = slice(2 * GB * g, 2 * GB * (g + 1))
                act.wait_ge(s_g, g + 1)
                act.activation(rz[:, cs, :].rearrange("r (j c) k -> r j c k", j=2), gates(g)[:, :, :, 0:2 * F],
                               ACT.Sigmoid).then_inc(s_sig, 1)
                act.wait_ge(s_gn, 2 * g + 2)
                act.activation(ya[:, cs, :], ya[:, cs, :], ACT.Tanh).then_inc(s_n, 1)
            act.wait_ge(s_var, 2)
            act.activation(st[2][:], st[1][:], ACT.Sqrt, bias=eps[:, 0:1], scale=1.0 / F).then_inc(s_a, 1)

        @block.tensor
        def _(pe):
            def sums(k):
                l = L[k]
                W = ZW if k == 0 else P

                H = H_PE[k]

                def pick_rows(b):
                    pe.wait_ge(l["cand"], b + 1)
                    for c in range(TC):
                        if c < TC_DVE:
                            pe.wait_ge(l["pick"], TC_DVE * b + c + 1)
                        else:
                            pe.wait_ge(l["pick_act"], TC_ACT * b + c - TC_DVE + 2)
                        for t in range(H):
                            for part in range(2):
                                mm = pe.matmul(psN[:, t // 2, t % 2 * NG * F:(t % 2 + 1) * NG * F],
                                               pick[k][:, c, t * P:(t + 1) * P],
                                               table_p[part][:, c * NG * F:(c + 1) * NG * F],
                                               start=(c == 0 and part == 0 and t % 2 == 0),
                                               stop=(c == TC - 1 and part == 1), skip_group_check=True)
                        mm.then_inc(l["picked"], 1)

                def flush_transposes(w):
                    pe.wait_ge(l["mS"], w + 1)
                    if k == 0:
                        for c in range(2):
                            pe.transpose(psT[:, c * P:c * P + P], sumS[:, c * P:c * P + P], ident[:])
                        pe.transpose(psT[0:F + 1, 2 * P:3 * P], sumS[:, K2:ZW], ident[:]).then_inc(l["tp"], 1)
                    else:
                        pe.matmul(psT[:, 0:P], sumS[:, 0:P], ident[:], start=True, stop=False)
                        pe.matmul(psT[:, 0:P], sumS[:, P:2 * P], ident[:], start=False, stop=True).then_inc(l["tp"], 1)

                def flush_result(w):
                    pe.wait_ge(l["tS"], 2 * w + 2)
                    pe.wait_ge(l["acc"], w + 2)
                    if k == 0:
                        for c in range(2):
                            pe.matmul(psR[0:F + 1, 0:P], W0[:, c, :], sumT[:, c, :], start=(c == 0), stop=False)
                        pe.matmul(psR[0:F + 1, 0:P], W0[0:F + 1, 2, :], sumT[0:F + 1, 2, :],
                                  start=False, stop=True).then_inc(l["res"], 1)
                    else:
                        pe.matmul(psR[0:ROWS1, 0:P], A1[:], sumT[:, 0, :], start=True, stop=True).then_inc(l["res"], 1)

                def body(b, buf, r):
                    cut = chunk_cols(k)

                    def window(w, q):
                        flush_transposes(w)
                        pe.wait_ge(l["match"], w + 1)
                        for n, j in enumerate(ORDER):
                            pe.wait_ge(l["z"], CREDIT + NCH * b + n + 1)
                            if k == 0:
                                pe.wait_ge(l["x"], CREDIT + NCH * b + n + 1)
                            if j in SPLIT[k]:
                                part_at = parts_of(k, j).start - cut[j]
                                if k == 0:
                                    pe.wait_ge(l["lo"], 2 * b + SPLIT[0].index(j) + 1)
                                else:
                                    pe.wait_ge(l["zh"], b + 1)
                                for g in range(cut[j], cut[j + 1]):
                                    for n_part, part in enumerate(z_part[0] if k == 0 else [z_both]):
                                        WR = ZS if k == 0 else 2 * P
                                        pe.matmul(psM[:, 0:WR], onehot_r[:, g, :], part[:, g + part_at, 0:WR],
                                                  start=(n == 0 and g == cut[j] and n_part == 0), stop=False)
                                continue
                            for g in range(cut[j], cut[j + 1]):
                                mm = pe.matmul(psM[:, 0:W], onehot[:, g, :], z[k][buf][:, g, 0:W],
                                               start=False, stop=(n == NCH - 1 and g == cut[j + 1] - 1))
                        mm.then_inc(l["mm"], 1)
                        flush_result(w)
                    for_each_window(pe, *windows_of(pe, b), window)
                    if not (isinstance(b, int) and b + 2 >= NB):
                        pick_rows(b + 2)

                pe.wait_ge(s_split, k + 1)
                pick_rows(0)
                pick_rows(1)
                if k == 0:
                    pe.wait_ge(s_w, N_W)
                    pe.wait_ge(s_meta, 1)
                for_each_block(pe, body, peeled=3)
                w = windows_in_all(pe)
                flush_transposes(w)
                flush_result(w)

            pe.wait_ge(s_const, 3)
            sums(0)
            pe.wait_ge(s_agg[0], 1)
            for g in range(5):
                for c in range(20 * g, 20 * g + 20):
                    t = pe.transpose(psN[0:R, g, (c - 20 * g) * (F + 1):(c - 20 * g + 1) * (F + 1)],
                                     cols(nodeT[0:F + 1, :], c), ident[0:F + 1, 0:F + 1])
                t.then_inc(s_nt, 1)
            pe.wait_ge(s_hs, 1)
            for g in range(C // 4):
                if g >= 5:
                    pe.wait_ge(s_hc, g - 4)
                for c in range(4 * g, 4 * g + 4):
                    t = pe.transpose(psN[0:2 * F, g % 5, (c - 4 * g) * R:(c - 4 * g + 1) * R],
                                     h_pad[:, c, :], ident[0:R, 0:R])
                t.then_inc(s_ht, 1)
            pe.wait_ge(s_hc, C // 4)
            sums(1)
            pe.wait_ge(s_agg[1], 1)
            for g in range(n_gate):
                if g >= 2:
                    pe.wait_ge(s_sig, g - 1)
                    pe.wait_ge(s_gn, 2 * (g - 1))
                for c in range(2 * GB * g, 2 * GB * (g + 1)):
                    j, i = divmod(c - 2 * GB * g, GB)
                    t = pe.matmul(psN[0:R, g % 2 * 2 + j, i * GS:i * GS + GW],
                                  cols(nodeT, c), gate_w[:], start=True, stop=True)
                t.then_inc(s_g, 1)

        @block.vector
        def _(dve):
            steps = [0]

            def step(ins):
                steps[0] += 1
                ins.then_inc(s_v, 1)
                dve.wait_ge(s_v, steps[0])

            def bc(t, n):
                return t.unsqueeze(2).to_broadcast([t.shape[0], t.shape[1], n])

            def aggregate(k):
                l = L[k]
                p0, p1 = (0, F + 1) if k == 0 else (AGG1, ROWS1)
                H, cut = H_PE[k], chunk_cols(k)
                gp = G - H
                at1, at2 = (dve.alloc_register(f"window_at{k}_{j}") for j in range(2))
                dve.reg_mov(at1, 0)
                dve.reg_mov(at2, 0)

                def add_window(w, at):
                    dve.wait_ge(l["res"], w + 1)
                    dve.wait_ge(l["acc"], w + 1)
                    v = nodeT[p0:p1, bass.ds(dve.snap(at, min_val=0, max_val=N - 1), P)]
                    dve.tensor_tensor(v, v, psR[p0:p1, 0:P], ALU.add).then_inc(l["acc"], 1)

                def pick_columns(b, buf, r):
                    dve.wait_ge(l["src"][buf], 32 * (r + 1))
                    dve.tensor_tensor(grp_hot[buf][:, 0:H, :], col_f[:, 0:NG].unsqueeze(1).to_broadcast([P, H, NG]),
                                      bc(grp[buf][:, 0:H], NG), ALU.is_equal).then_inc(l["hot_g"], 1)
                    for c in range(TC_DVE):
                        dve.wait_ge(l["picked"], TC * b + c + 1)
                        dve.tensor_scalar(pick[k][:, c, 0:H * P], src_mod[buf][:, 0:H * P],
                                          chunk_node[:, c:c + 1], None, ALU.is_equal).then_inc(l["pick"], 1)

                def mask_candidates(b, buf):
                    dve.wait_ge(l["hot_g"], b + 1)
                    dve.wait_ge(l["picked"], TC * (b + 2))
                    for t0, t1 in ((0, H // 2 * 2), (H // 2 * 2, H)):
                        if t1 > t0:
                            nbank, m = -(-(t1 - t0) // 2), min(t1 - t0, 2) * NG
                            last = dve.tensor_tensor(
                                cand[k][:, t0:t1].rearrange("p t g f -> p (t g) f").rearrange("p (k m) f -> p k m f", m=m),
                                psN[:, t0 // 2:t0 // 2 + nbank, 0:m * F].rearrange("p k (m f) -> p k m f", f=F),
                                grp_hot[buf][:, t0:t1].rearrange("p t g -> p (t g)").rearrange("p (k m) -> p k m", m=m)
                                .unsqueeze(3).to_broadcast([P, nbank, m, F]), ALU.mult)
                    last.then_inc(l["cand"], 1)

                def sum_candidates(b, buf):
                    dve.wait_ge(l["cand"], b + 2)
                    if k == 0:
                        dve.wait_ge(l["x"], NCH * b + 1)
                    dve.tensor_reduce(xs[buf][:, gp:G, :], cand[k][:, 0:H].rearrange("p t g f -> p t f g"),
                                      AX.X, ALU.add).then_inc(l["sel"], 1)

                def body(b, buf, r):
                    first, n_win = windows_of(dve, b)
                    dve.wait_ge(l["inp"][buf], 64 * (r + 1))
                    dve.wait_ge(l["rel"], b + first + 1)
                    dve.tensor_scalar(rel[:], dstb[buf][:], lo_f[:, bass.ds(b, 1)], None, ALU.subtract).then_inc(l["rel"], 1)
                    if k == 1:
                        dve.tensor_tensor(typ_hot[:], col_f[:, 0:T].unsqueeze(1).to_broadcast([P, G, T]),
                                          bc(typ[buf], T), ALU.is_equal).then_inc(l["hot"], 1)
                        dve.wait_ge(l["hot"], b + 1)
                    coef, n = (eab[buf], F) if k == 0 else (typ_hot, T)
                    lo = dve.value_load(span_row[0:1, bass.ds(b, 1), 0:1].rearrange("p a b -> p (a b)"),
                                        min_val=0, max_val=N - 1)

                    def window(w, q):
                        dve.wait_ge(l["mm"], w + 1)
                        dve.wait_ge(l["rel"], b + w + 2)
                        dve.tensor_tensor(onehot_r[:], col_f[:].unsqueeze(1).to_broadcast([P, G, P]),
                                          bc(rel, P), ALU.is_equal).then_inc(l["match"], 1)
                        dve.wait_ge(l["match"], w + 1)
                        dve.tensor_scalar(rel[:], rel[:], float(P), None, ALU.subtract).then_inc(l["rel"], 1)
                        add_window(w, at2)
                        dve.reg_mov(at2, dve.snap(at1, min_val=0, max_val=N - 1))
                        dve.reg_mov(at1, lo + q * P)

                    def outer(out_z, j, rows):
                        m = cut[j + 1] - cut[j]
                        return dve.tensor_tensor(
                            out_z.rearrange("p g (k i) -> p g k i", i=F),
                            coef[:, cut[j]:cut[j + 1], :].unsqueeze(3).to_broadcast([P, m, n, F]),
                            rows.unsqueeze(2).to_broadcast([P, m, n, F]), ALU.mult)

                    def low_part(j):
                        dve.wait_ge(l["hi"], 2 * b + SPLIT[0].index(j) + 1)
                        at = parts_of(0, j)
                        dve.tensor_tensor(z_part[0][1][:, at, :], z[0][buf][:, cut[j]:cut[j + 1], :],
                                          z_part[0][0][:, at, :], ALU.subtract).then_inc(l["lo"], 1)

                    if k == 0:
                        dve.wait_ge(l["sel"], b + 1)
                        outer(z[0][buf][:, gp:G, 0:K2], NCH - 1, xs[buf][:, gp:G, :]).then_inc(l["z"], 1)
                        window(first, 0)
                        low_part(NCH - 1)
                    else:
                        dve.wait_ge(l["hi"], b + 1)
                        dve.tensor_tensor(x_lo, xs[buf][:, gp:G, :], x_hi, ALU.subtract).then_inc(l["lo"], 1)
                        window(first, 0)
                        outer(z_part[1][0], NCH - 1, x_hi).then_inc(l["zh"], 1)
                        dve.wait_ge(l["lo"], b + 1)
                        outer(z_part[1][1], NCH - 1, x_lo).then_inc(l["z"], 1)
                    for j in ORDER[1:]:
                        dve.wait_ge(l["got"][buf][j], 16 * (cut[j + 1] - cut[j]) * (r + 1))
                        outer(z[k][buf][:, cut[j]:cut[j + 1], 0:n * F], j, xs[buf][:, cut[j]:cut[j + 1], :]).then_inc(l["z"], 1)
                        if k == 0 and j == ORDER[2]:
                            low_part(ORDER[1])
                    with dve.If(n_win > 1):
                        with dve.Fori(1, n_win) as q:
                            window(first + q, q)
                    if not (isinstance(b, int) and b + 1 >= NB):
                        mask_candidates(b + 1, 1 - buf)
                    if not (isinstance(b, int) and b + 2 >= NB):
                        pick_columns(b + 2, buf, r + 1)
                    if not (isinstance(b, int) and b + 1 >= NB):
                        sum_candidates(b + 1, 1 - buf)

                pick_columns(0, 0, 0)
                dve.wait_ge(s_tab[k], N_TAB)
                rows = table[:].rearrange("p c g f -> p (c g f)")
                step(dve.tensor_copy(table_p[0][:], rows))
                step(dve.tensor_tensor(table_p[1][:], rows, table_p[0][:], ALU.subtract))
                dve.sem_inc(s_split, 1)
                if k == 0:
                    before_blocks()
                mask_candidates(0, 0)
                pick_columns(1, 1, 0)
                sum_candidates(0, 0)
                for_each_block(dve, body, peeled=3)
                last = windows_in_all(dve)
                add_window(last, at2)
                add_window(last + 1, at1)
                dve.wait_ge(l["acc"], last + 3)
                dve.sem_inc(s_agg[k], 1)

            def centre_and_square():
                step(dve.tensor_scalar(st[0][:], st[0][:], 1.0 / F, None, ALU.mult))
                step(dve.tensor_tensor(yb[:], ya[:], bc(st[0], F), ALU.subtract))
                step(dve.tensor_tensor(ya[:], yb[:], yb[:], ALU.mult))
                step(dve.tensor_reduce(st[1][:], ya[:], AX.X, ALU.add))
                dve.sem_inc(s_var, 1)

            for l in L:
                dve.sem_inc(l["z"], CREDIT)
                dve.sem_inc(l["picked"], TC)
                dve.sem_inc(l["pick_act"], 1)
                dve.sem_inc(l["cand"], 1)
                dve.sem_inc(l["mm"], 1)
                dve.sem_inc(l["acc"], 1)
                dve.sem_inc(l["rel"], 1)
            step(dve.memset(zero[:], 0.0))
            dve.sem_inc(s_zero, 1)
            step(dve.memset(table[:], 0.0))
            dve.sem_inc(s_init, 1)
            dve.wait_ge(s_const, 4)
            step(dve.tensor_copy(chunk_node[:], chunk_node_i[:]))
            step(dve.tensor_scalar(neg_node[:], chunk_node[:], -1.0, None, ALU.mult))
            step(dve.memset(one[:], 1.0))
            dve.sem_inc(s_node, 1)
            step(dve.tensor_copy(col_f[:], col_i[:]))
            dve.wait_ge(s_sr, 16)
            step(dve.tensor_scalar(src_q, src_rows, LOG_P, None, ALU.arith_shift_right))
            step(dve.tensor_scalar(src_q, src_q, float(DIV_MUL), None, ALU.mult))
            step(dve.tensor_scalar(src_g, src_q, DIV_SHIFT, None, ALU.arith_shift_right))
            step(dve.tensor_scalar(src_v, src_g, float(-GRP), None, ALU.mult))
            step(dve.tensor_tensor(src_v, src_v, src_rows, ALU.add))
            for k in range(2):
                m = P * H_PE[k]
                step(dve.tensor_copy(src_out[k].rearrange("b (t p) -> b t p", p=P),
                                     src_v[:, n_src - m:n_src].rearrange("b (p t) -> b t p", p=P)))
            dve.sem_inc(s_mod, 1)
            step(dve.memset(W0[:], 0.0))
            step(dve.memset(W0[0:1, 2, F:F + 1], 1.0))
            step(dve.memset(A1[:], 0.0))
            step(dve.memset(gate_w[:], 0.0))
            dve.sem_inc(s_w0z, 1)
            dve.wait_ge(s_dr, 32)
            step(dve.tensor_reduce(span[:, 0:1], dst_rows[:], AX.X, ALU.min))
            step(dve.tensor_reduce(span_hi[:], dst_rows[:], AX.X, ALU.max))
            step(dve.tensor_tensor(span_hi[:], span_hi[:], span[:, 0:1], ALU.subtract))
            step(dve.tensor_scalar(span_hi[:], span_hi[:], LOG_P, None, ALU.arith_shift_right))
            step(dve.tensor_scalar(span[:, 1:2], span_hi[:], 1.0, None, ALU.add))
            dve.sem_inc(s_span, 1)

            def before_blocks():
                step(dve.memset(ones_row[:], 1.0))
                step(dve.memset(win_sum[:], 0.0))
                step(dve.memset(sumS[:], 0.0))
                dve.sem_inc(L[0]["mS"], 1)
                step(dve.memset(psR[:], 0.0))
                dve.sem_inc(L[0]["res"], 1)
                dve.wait_ge(s_spr, 32)
                step(dve.tensor_copy(win_f[:], span_row[0:1, :, 1]))
                step(dve.tensor_copy(lo_f[:], lo_i[:, :, 0]))
                step(dve.tensor_tensor_scan(win_sum[:, 1:NB + 1], ones_row[:], win_f[:], 0.0, ALU.mult, ALU.add))
                step(dve.tensor_copy(win_first[:], win_sum[:]))
                for b in range(2):
                    step(dve.memset(z[0][b][:, :, K2:K2 + 1], 1.0))
                    step(dve.memset(z[0][b][:, :, ZW:ZS], 0.0))
                dve.sem_inc(s_meta, 1)
                step(dve.memset(eps[:], 1e-5))
                dve.wait_ge(s_nz, 1)
                dve.wait_ge(s_w, N_W)
                step(dve.tensor_tensor(h[:], h[:], bias_b[:].unsqueeze(1).to_broadcast([R, C, F]), ALU.add))

            aggregate(0)

            step(dve.memset(h_pad[:, :, F:2 * F], 0.0))
            step(dve.memset(h_pad[:, :, F:F + 2], 1.0))
            for g in range(5):
                dve.wait_ge(s_nt, g + 1)
                v = psN[0:R, g, 0:20 * (F + 1)].rearrange("r (c f) -> r c f", f=F + 1)
                cs = slice(20 * g, 20 * g + 20)
                step(dve.tensor_scalar(st[0][:, cs], v[:, :, F], 1.0, None, ALU.max))
                step(dve.reciprocal(st[0][:, cs], st[0][:, cs]))
                step(dve.tensor_tensor(ya[:, cs, :], v[:, :, 0:F], bc(st[0][:, cs], F), ALU.mult))
                step(dve.tensor_tensor(ya[:, cs, :], ya[:, cs, :], h[:, cs, :], ALU.add))
                step(dve.tensor_reduce(st[0][:, cs], ya[:, cs, :], AX.X, ALU.add))
            centre_and_square()
            dve.wait_ge(s_a, 1)
            step(dve.reciprocal(st[3][:], st[2][:]))
            step(dve.tensor_tensor(yb[:], yb[:], bc(st[3], F), ALU.mult))
            dve.sem_inc(s_h, 1)
            step(dve.tensor_copy(h_pad[:, :, 0:F], yb[:]))
            dve.sem_inc(s_hs, 1)
            step(dve.tensor_copy(h[:], yb[:]))
            step(dve.memset(sumS[:], 0.0))
            step(dve.memset(psR[:], 0.0))
            dve.sem_inc(L[1]["res"], 1)
            dve.sem_inc(L[1]["mS"], 1)

            aggregate(1)

            def gru_tail(g):
                cs = slice(2 * GB * g, 2 * GB * (g + 1))
                hv, n, zh = h[:, cs, :], ya[:, cs, :], yb[:, cs, :]
                dve.wait_ge(s_n, g + 1)
                step(dve.tensor_tensor(zh, hv, n, ALU.subtract))
                step(dve.tensor_tensor(zh, zh, rz[:, cs, F:2 * F], ALU.mult))
                step(dve.tensor_tensor(n, n, hv, ALU.add))
                step(dve.tensor_tensor(n, n, zh, ALU.add))
                step(dve.tensor_reduce(st[0][:, cs], n, AX.X, ALU.add))

            for g in range(n_gate):
                cs = slice(2 * GB * g, 2 * GB * (g + 1))
                two = lambda t: t.rearrange("r (j c) k -> r j c k", j=2)
                dve.wait_ge(s_sig, g + 1)
                dve.tensor_tensor(two(ya[:, cs, :]), two(rz[:, cs, 0:F]), gates(g)[:, :, :, 3 * F:GC], ALU.mult).then_inc(s_gn, 1)
                dve.wait_ge(s_gn, 2 * g + 1)
                dve.tensor_tensor(two(ya[:, cs, :]), two(ya[:, cs, :]), gates(g)[:, :, :, 2 * F:3 * F], ALU.add).then_inc(s_gn, 1)
                if g:
                    gru_tail(g - 1)
            gru_tail(n_gate - 1)
            centre_and_square()
            dve.wait_ge(s_a, 2)
            step(dve.reciprocal(st[3][:], st[2][:]))
            dve.tensor_tensor(yb[:], yb[:], bc(st[3], F), ALU.mult).then_inc(s_out, 1)


_INS = ["x", "src", "dst", "edge_attr_16", "edge_type_8", "W_e", "b_e", "bias", "A_t", "w_ihT", "w_hhT", "b_ih", "b_hh"]


def kernel(x, src, dst, edge_attr_16, edge_type_8, L0_gnn_W_e, L0_gnn_b_e, L0_gnn_bias, L1_gnn_edge_emb,
           L1_gnn_w_ih, L1_gnn_w_hh, L1_gnn_b_ih, L1_gnn_b_hh):
    import numpy as np
    import concourse.bacc as bacc
    from concourse.bass_utils import run_bass_kernel_spmd

    n_types = L1_gnn_edge_emb.shape[0]
    given = dict(
        x=x, src=src, dst=dst, edge_attr_16=edge_attr_16, edge_type_8=edge_type_8,
        W_e=np.asarray(L0_gnn_W_e).reshape(K2, F), b_e=np.asarray(L0_gnn_b_e).reshape(F, F),
        bias=np.asarray(L0_gnn_bias).reshape(1, F),
        A_t=np.asarray(L1_gnn_edge_emb).reshape(n_types, F, F).transpose(0, 2, 1).reshape(n_types * F, F),
        w_ihT=np.asarray(L1_gnn_w_ih).T, w_hhT=np.asarray(L1_gnn_w_hh).T,
        b_ih=np.asarray(L1_gnn_b_ih).reshape(1, 3 * F), b_hh=np.asarray(L1_gnn_b_hh).reshape(1, 3 * F))
    nc = bacc.Bacc("TRN2", target_bir_lowering=False, num_devices=1)
    arrays, args = {}, []
    for name in _INS:
        a = np.ascontiguousarray(given[name])
        arrays[f"in_{name}"] = a
        args.append(nc.dram_tensor(f"in_{name}", a.shape, mybir.dt.from_np(a.dtype), kind="ExternalInput").ap())
    args.append(nc.dram_tensor("out_0", x.shape, F32, kind="ExternalOutput").ap())
    build(nc, *args)
    r = run_bass_kernel_spmd(nc, [arrays], core_ids=[0])
    return r.results[0]["out_0"]
```
